# Optimizing a Trainium2 kernel written in Bass

```python
import numpy as np
import jax
import jax.numpy as jnp

def _softmax(x, axis=-1):
    return jax.nn.softmax(x, axis=axis)

def _gelu(x):
    return jax.nn.gelu(x, approximate=True)

def _silu(x):
    return jax.nn.silu(x)

def _sigmoid(x):
    return jax.nn.sigmoid(x)

def _layernorm(x, axis=-1, eps=1e-05):
    m = jnp.mean(x, axis=axis, keepdims=True)
    v = jnp.var(x, axis=axis, keepdims=True)
    return (x - m) / jnp.sqrt(v + eps)

def _scatter_add(tgt, idx, src, axis=0):
    return tgt.at[idx].add(src)

def _segment_sum(src, seg, n):
    return jax.ops.segment_sum(src, seg, n)
kernel_name = 'mk_cond_resid_d4_seqx_r8_c1acda'

def setup_inputs(seed: int=0):
    np.random.seed(seed)
    _w = jnp.asarray

    def _rec_inputs():
        import jax
        import jax.numpy as jnp
        _rk = jax.random.key(seed)
        x = -7.109e-05 + 0.9999 * jax.random.normal(jax.random.fold_in(_rk, 1), (32, 32, 512), jnp.float32)
        _lenS = 32 - jax.random.randint(jax.random.fold_in(_rk, 7), (32,), 0, max(1, 32 // 4) + 1, jnp.int32)
        _lenS2 = 32 - jax.random.randint(jax.random.fold_in(_rk, 8), (32,), 0, max(1, 32 // 4) + 1, jnp.int32)
        itok_B_0_15 = jax.random.randint(jax.random.fold_in(_rk, 11), (32,), 0, 16, jnp.int32)
        itok_B_0_23 = jax.random.randint(jax.random.fold_in(_rk, 12), (32,), 0, 24, jnp.int32)
        itok_B_0_7 = jax.random.randint(jax.random.fold_in(_rk, 13), (32,), 0, 8, jnp.int32)
        itok_B_8_3872 = jax.random.randint(jax.random.fold_in(_rk, 14), (32,), 8, 3873, jnp.int32)
        return (x, itok_B_0_15, itok_B_0_23, itok_B_0_7, itok_B_8_3872)
    x, itok_B_0_15, itok_B_0_23, itok_B_0_7, itok_B_8_3872 = _rec_inputs()

    def _L0_cond_setup():
        import jax, jax.numpy as jnp
        import numpy as np
        NUM_CONDITIONS = 16
        IN_CH = 32
        OUT_CH = 32
        B = 64
        T = 512
        key = jax.random.key(seed)
        k_x, k_w, k_c = jax.random.split(key, 3)
        x = jax.random.normal(k_x, (B, IN_CH, T), dtype=jnp.float32)
        bound = float(np.sqrt(6.0 / IN_CH))
        weights = jax.random.uniform(k_w, (NUM_CONDITIONS, IN_CH, OUT_CH), dtype=jnp.float32, minval=-bound, maxval=bound)
        condition = jax.random.randint(k_c, (B,), 0, NUM_CONDITIONS, dtype=jnp.int64)
        return {'x': x, 'weights': weights, 'condition': condition}
    _L0_cond_all = _L0_cond_setup()
    _L0_cond_in = {k: v for k, v in _L0_cond_all.items() if k in ('weights',)}
    del _L0_cond_all

    def _L1_cond_setup():
        import jax, jax.numpy as jnp
        import numpy as np
        R = 16
        ALPHA = 32
        SCALING = ALPHA / R
        SLOTS = 32
        IN_F = 512
        OUT_F = 512
        B, T = (8, 128)
        key = jax.random.key(seed)
        k1, k2, k3, k4, k5, k6 = jax.random.split(key, 6)
        x = jax.random.normal(k1, (B, T, IN_F), dtype=jnp.float32)
        adapter_mapping = jax.random.randint(k2, (B,), 0, SLOTS, dtype=jnp.int32)
        W = jax.random.normal(k3, (OUT_F, IN_F), dtype=jnp.float32) * 0.02
        b = jax.random.normal(k4, (OUT_F,), dtype=jnp.float32) * 0.02
        lora_As = jax.random.normal(k5, (SLOTS, IN_F, R), dtype=jnp.float32) * 0.02
        lora_Bs = jax.random.normal(k6, (SLOTS, R, OUT_F), dtype=jnp.float32) * 0.02
        return {'x': x, 'adapter_mapping': adapter_mapping, 'W': W, 'b': b, 'lora_As': lora_As, 'lora_Bs': lora_Bs}
    _L1_cond_all = _L1_cond_setup()
    _L1_cond_in = {k: v for k, v in _L1_cond_all.items() if k in ('W', 'b', 'lora_As', 'lora_Bs')}
    del _L1_cond_all

    def _L2_cond_setup():
        import jax, jax.numpy as jnp
        import numpy as np
        TOP_K = 2
        LANG_BIAS = 5.0
        SCALING = 32.0 / 16.0
        LANGUAGE_PAD_ID = -1
        key = jax.random.key(seed)
        ks = jax.random.split(key, 6)
        B, T, D, O, E, R = (4, 256, 512, 512, 8, 16)
        x = jax.random.normal(ks[0], (B, T, D), dtype=jnp.float32)
        language_ids = jax.random.randint(ks[1], (B,), 0, E).astype(jnp.int64)
        W = jax.random.normal(ks[2], (O, D), dtype=jnp.float32) * (1.0 / np.sqrt(D))
        Wr = jax.random.normal(ks[3], (E, D), dtype=jnp.float32) * (1.0 / np.sqrt(D))
        A = jax.random.normal(ks[4], (E, R, D), dtype=jnp.float32) * (1.0 / np.sqrt(D))
        Bm = jax.random.normal(ks[5], (O, R), dtype=jnp.float32) * 0.0
        Bm = jnp.broadcast_to(Bm, (E, O, R)) + jax.random.normal(ks[5], (E, O, R), dtype=jnp.float32) * 0.02
        return {'x': x, 'language_ids': language_ids, 'W': W, 'Wr': Wr, 'A': A, 'B': Bm}
    _L2_cond_all = _L2_cond_setup()
    _L2_cond_in = {k: v for k, v in _L2_cond_all.items() if k in ('W', 'Wr', 'A', 'B')}
    del _L2_cond_all

    def _L3_cond_setup():
        import math
        import jax, jax.numpy as jnp
        import numpy as np
        H, N, B, L = (32, 64, 16, 512)
        DT_MIN, DT_MAX = (0.001, 0.1)

        def _get_kernel(log_dt, C, log_A_real, A_imag, length):
            Cc = C[..., 0] + 1j * C[..., 1]
            dt = jnp.exp(log_dt)
            A = -jnp.exp(log_A_real) + 1j * A_imag
            dtA = A * dt[:, None]
            P = dtA[:, :, None] * jnp.arange(length, dtype=jnp.float32)
            Cs = Cc * (jnp.exp(dtA) - 1.0) / A
            K = 2.0 * jnp.einsum('hn,hnl->hl', Cs, jnp.exp(P)).real
            return K
        key = jax.random.key(seed)
        ks = jax.random.split(key, 6)
        u = jax.random.normal(ks[0], (B, H, L), dtype=jnp.float32)
        length = jax.random.randint(ks[1], (B,), 0, L)
        log_dt = jax.random.uniform(ks[2], (H,), dtype=jnp.float32) * (math.log(DT_MAX) - math.log(DT_MIN)) + math.log(DT_MIN)
        C = jax.random.normal(ks[3], (H, N, 2), dtype=jnp.float32)
        log_A_real = jnp.log(0.5 * jnp.ones((H, N), dtype=jnp.float32))
        A_imag = math.pi * jnp.broadcast_to(jnp.arange(N, dtype=jnp.float32), (H, N))
        D = jax.random.normal(ks[4], (H,), dtype=jnp.float32)
        return {'u': u, 'length': length, 'log_dt': log_dt, 'C': C, 'log_A_real': log_A_real, 'A_imag': A_imag, 'D': D}
    _L3_cond_all = _L3_cond_setup()
    _L3_cond_in = {k: v for k, v in _L3_cond_all.items() if k in ('log_dt', 'C', 'log_A_real', 'A_imag', 'D')}
    del _L3_cond_all
    return {'x': x, 'itok_B_0_15': itok_B_0_15, 'itok_B_0_23': itok_B_0_23, 'itok_B_0_7': itok_B_0_7, 'itok_B_8_3872': itok_B_8_3872, 'L0_cond_weights': _L0_cond_in['weights'], 'L1_cond_W': _L1_cond_in['W'], 'L1_cond_b': _L1_cond_in['b'], 'L1_cond_lora_As': _L1_cond_in['lora_As'], 'L1_cond_lora_Bs': _L1_cond_in['lora_Bs'], 'L2_cond_W': _L2_cond_in['W'], 'L2_cond_Wr': _L2_cond_in['Wr'], 'L2_cond_A': _L2_cond_in['A'], 'L2_cond_B': _L2_cond_in['B'], 'L3_cond_log_dt': _L3_cond_in['log_dt'], 'L3_cond_C': _L3_cond_in['C'], 'L3_cond_log_A_real': _L3_cond_in['log_A_real'], 'L3_cond_A_imag': _L3_cond_in['A_imag'], 'L3_cond_D': _L3_cond_in['D']}

def reference(x, itok_B_0_15, itok_B_0_23, itok_B_0_7, itok_B_8_3872, L0_cond_weights, L1_cond_W, L1_cond_b, L1_cond_lora_As, L1_cond_lora_Bs, L2_cond_W, L2_cond_Wr, L2_cond_A, L2_cond_B, L3_cond_log_dt, L3_cond_C, L3_cond_log_A_real, L3_cond_A_imag, L3_cond_D):
    import jax
    import jax.numpy as jnp

    def _L0_cond_ref(x, weights, condition):
        import jax, jax.numpy as jnp
        import numpy as np
        NUM_CONDITIONS = 16
        IN_CH = 32
        OUT_CH = 32
        B = 64
        T = 512
        W = weights[condition]
        return jnp.einsum('bct,bcd->bdt', x, W)

    def _L1_cond_ref(x, adapter_mapping, W, b, lora_As, lora_Bs):
        import jax, jax.numpy as jnp
        import numpy as np
        R = 16
        ALPHA = 32
        SCALING = ALPHA / R
        SLOTS = 32
        IN_F = 512
        OUT_F = 512
        B, T = (8, 128)
        base_out = jnp.einsum('bti,oi->bto', x, W) + b
        A = lora_As[adapter_mapping]
        Bm = lora_Bs[adapter_mapping]
        lora_h = jnp.einsum('bti,bir->btr', x, A)
        lora_out = jnp.einsum('btr,bro->bto', lora_h, Bm)
        return base_out + lora_out * SCALING

    def _L2_cond_ref(x, language_ids, W, Wr, A, B):
        import jax, jax.numpy as jnp
        import numpy as np
        TOP_K = 2
        LANG_BIAS = 5.0
        SCALING = 32.0 / 16.0
        LANGUAGE_PAD_ID = -1
        base = jnp.einsum('btd,od->bto', x, W)
        E = Wr.shape[0]
        logits = jnp.einsum('btd,ed->bte', x.astype(jnp.float32), Wr.astype(jnp.float32))
        expert_targets = language_ids
        valid = expert_targets >= 0
        tgt = jnp.where(valid, expert_targets, 0)
        bias = jax.nn.one_hot(tgt, E, dtype=logits.dtype) * LANG_BIAS
        bias = jnp.where(valid[:, None], bias, 0.0)
        logits = logits + bias[:, None, :]
        topw, topi = jax.lax.top_k(logits, TOP_K)
        weights = jax.nn.softmax(topw, axis=-1)
        gates = jnp.sum(jax.nn.one_hot(topi, E, dtype=weights.dtype) * weights[..., None], axis=-2)
        gates = gates.astype(x.dtype)
        h = jnp.einsum('btd,erd->bter', x, A)
        lora_out = jnp.einsum('bter,bte,eor->bto', h, gates, B)
        return base + SCALING * lora_out

    def _L3_cond_ref(u, length, log_dt, C, log_A_real, A_imag, D):
        import math
        import jax, jax.numpy as jnp
        import numpy as np
        H, N, B, L = (32, 64, 16, 512)
        DT_MIN, DT_MAX = (0.001, 0.1)

        def _get_kernel(log_dt, C, log_A_real, A_imag, length):
            Cc = C[..., 0] + 1j * C[..., 1]
            dt = jnp.exp(log_dt)
            A = -jnp.exp(log_A_real) + 1j * A_imag
            dtA = A * dt[:, None]
            P = dtA[:, :, None] * jnp.arange(length, dtype=jnp.float32)
            Cs = Cc * (jnp.exp(dtA) - 1.0) / A
            K = 2.0 * jnp.einsum('hn,hnl->hl', Cs, jnp.exp(P)).real
            return K
        Bq, Hq, Lq = u.shape
        mask = (jnp.arange(Lq) < length[:, None]).astype(u.dtype)
        u_m = u * mask[:, None, :]
        kernel = _get_kernel(log_dt, C, log_A_real, A_imag, Lq)
        n = 2 * Lq
        k_f = jnp.fft.rfft(kernel, n=n)
        u_f = jnp.fft.rfft(u_m, n=n)
        y = jnp.fft.irfft(u_f * k_f, n=n)[..., :Lq]
        y = y + u_m * D[:, None]
        return y * mask[:, None, :]
    x = x + _L0_cond_ref(x, L0_cond_weights, itok_B_0_15)
    x = x + _L1_cond_ref(x, itok_B_0_23, L1_cond_W, L1_cond_b, L1_cond_lora_As, L1_cond_lora_Bs)
    x = x + _L2_cond_ref(x, itok_B_0_7, L2_cond_W, L2_cond_Wr, L2_cond_A, L2_cond_B)
    x = x + _L3_cond_ref(x, itok_B_8_3872, L3_cond_log_dt, L3_cond_C, L3_cond_log_A_real, L3_cond_A_imag, L3_cond_D)
    return x

_drawn_inputs = setup_inputs


def setup_inputs(seed=0):
    import zlib

    import numpy as np

    out = dict(_drawn_inputs(seed))
    spreads = {'L3_cond_log_A_real': (-0.6931471824645996, 0.2)}
    factors = {'L1_cond_b': 5.905}
    for name, (base, spread) in spreads.items():
        noise = np.random.default_rng([zlib.crc32(name.encode()), seed]).standard_normal(out[name].shape)
        drawn = base * np.exp(spread * noise) if base else spread * noise
        out[name] = jnp.asarray(drawn.astype(out[name].dtype))
    for name, factor in factors.items():
        out[name] = (out[name] * factor).astype(out[name].dtype)
    return out
```

```python
import math
from contextlib import ExitStack

import numpy as np
import concourse.bass as bass
from concourse import mybir

F32 = mybir.dt.float32
F16 = mybir.dt.float16
I32 = mybir.dt.int32
U32 = mybir.dt.uint32
ALU = mybir.AluOpType
ACT = mybir.ActivationFunctionType

P = 128
WS = 64.0
PARTS_USED = [(0, 0), (1, 0), (0, 1)]

TWO_PI = 2.0 * math.pi
PI_DOWN = 3.1415925


def cut(value, bits):
    m, e = math.frexp(value)
    return math.ldexp(math.floor(math.ldexp(m, bits)), e - bits)


PI_HI = cut(TWO_PI, 8)
PI_MID = cut(TWO_PI - PI_HI, 11)
PI_LO = TWO_PI - PI_HI - PI_MID
LN2_HI = cut(math.log(2.0), 12)
LN2_LO = math.log(2.0) - LN2_HI
EXP_TERMS = 7


def cond_resid_kernel(nc, x, cond, slot, lang, length, W0, W1, b1, lora_A, lora_B,
                      W2, Wr, A2, B2, log_dt, C, log_A_real, A_imag, D, out):
    NB, NH, T = x.shape
    KC = T // P
    R = lora_A.shape[2]
    E = Wr.shape[0]
    N = A_imag.shape[1]
    NTOK = NB * NH
    G0 = P // NH
    NG0 = NB // G0
    GA = P // R
    NGA = NB // GA
    TA = GA * NH
    NT = NTOK // P
    HT = P // NB
    HALF = NTOK // 2
    LB = 32
    LA = T // LB
    NL = LB + LA
    NTAB = NH * NL
    AW = E * R + E
    KPAD = T + P
    assert 2 * N == P and E * R == P and T == KC * P and E == 8

    w0_dram = nc.dram_tensor("w0_rows", [NB, NH * NH], F32)
    la_dram = nc.dram_tensor("lora_a_rows", [NB, T * R], F32)
    lb_dram = nc.dram_tensor("lora_b_rows", [NB, R * T], F32)
    kern_dram = nc.dram_tensor("conv_kernels", [NH * 2, KPAD], F16)

    with ExitStack() as ctx:
        def sb(name, shape, dt=F32):
            return ctx.enter_context(nc.sbuf_tensor(name, shape, dt))

        def sem(name):
            return ctx.enter_context(nc.semaphore(name))

        ident = sb("ident", [P, P])
        w0_mask = sb("w0_mask", [P, G0, NH])
        lora_mask = sb("lora_mask", [P, GA, NH])
        steps = sb("steps", [P, T])
        powers_i = sb("powers_i", [P, NL], I32)
        powers = sb("powers", [P, NL])
        ids_i = sb("ids_i", [P, 2], I32)
        ids = sb("ids", [P, 2])
        gather_ids = sb("gather_ids", [NB, 2], I32)
        conv_mask = sb("conv_mask", [P, T])
        steps_i = conv_mask[:, :].bitcast(I32)
        lang_bias = sb("lang_bias", [P, E])
        bias_sb = sb("bias_sb", [P, KC])

        x_sb = sb("x_sb", [P, NG0, T])
        w0_blocks = sb("w0_blocks", [P, NG0, NH])
        w0_diag = sb("w0_diag", [P, NG0, P])
        w0_rows_sb = sb("w0_rows_sb", [P, NH * NH])
        w0_rows = w0_rows_sb[0:NB, :]
        w1t = sb("w1t", [P, 2, KC, T], F16)
        w2t = sb("w2t", [P, 2, KC, T], F16)
        awt = sb("awt", [P, 2, KC, AW], F16)
        b2t = sb("b2t", [P, 2, T], F16)
        la16 = sb("la16", [P, 2, KC, NB, R], F16)
        lb16 = sb("lb16", [P, 2, NGA, T], F16)
        xt16 = sb("xt16", [P, 2, KC, NTOK], F16)
        lora_h = sb("lora_h", [P, NGA, TA])
        lora_h16 = sb("lora_h16", [P, 2, NGA, TA], F16)
        x2_sb = sb("x2_sb", [P, 2, NH, NB // 2])
        x2t16 = sb("x2t16", [P, 2, KC, NH, NB], F16)
        toep = sb("toep", [P, NH, 2, T], F16)
        zeros16 = sb("zeros16", [2 * NH, P], F16)

        toep_flat = toep[:, :, :, :].rearrange("p h c t -> p (h c t)")
        ROW = 2 * T * R
        la_rows = toep_flat[0:NB, 0:ROW].bitcast(F32)
        lb_rows = toep_flat[0:NB, ROW:2 * ROW].bitcast(F32)

        arena = sb("arena", [P, KC * T + NB * KC * R + NGA * T])
        wide = [arena[:, 0:KC * T], arena[:, KC * T:KC * T + NB * KC * R], arena[:, KC * T + NB * KC * R:]]
        w1_nat = wide[0].rearrange("p (k i) -> p k i", k=KC)
        w2_nat = w1_nat
        out_sb = wide[0].rearrange("p (k i) -> p k i", i=T)
        la_sb = wide[1].rearrange("p (b j) -> p b j", b=NB)
        lb_sb = wide[2].rearrange("p (g o) -> p g o", g=NGA)

        def table(i):
            return arena[:, i * NTAB:(i + 1) * NTAB].rearrange("p (h l) -> p h l", h=NH)

        tab_th, tab_abs, tab_mag = table(0), table(1), table(2)
        tab_ki = table(3).bitcast(I32)

        x_flat = x_sb[:, :, :].rearrange("p g t -> p (g t)")
        trig_b = x_flat[:, 0:NH * LB].rearrange("p (h b) -> p h b", h=NH)
        cos_a = x_flat[:, NH * LB:NH * (LB + LA)].rearrange("p (h a) -> p h a", h=NH)
        sin_a = x_flat[:, NH * (LB + LA):NH * (LB + 2 * LA)].rearrange("p (h a) -> p h a", h=NH)
        K0 = NH * (LB + 2 * LA)
        k64 = x_flat[0:LA, K0:K0 + NH * LB].rearrange("a (h b) -> a h b", h=NH)
        k16 = x_flat[0:LA, K0 + NH * LB:K0 + 2 * NH * LB].bitcast(F16).rearrange("a (h c b) -> a h c b", h=NH, c=2)

        x2_flat = x2t16[:, :, :, :, :].rearrange("p c k h b -> p (c k h b)").bitcast(F32)
        a2_nat = x2_flat[:, 0:T]
        wr_nat = x2_flat[0:E, T:2 * T]
        b2_nat = x2_flat[:, 2 * T:3 * T].rearrange("p (k e r) -> p k e r", k=KC, e=E)
        zcat = x2_flat[0:NH, 3 * T:3 * T + 8 * N].rearrange("h (i c n) -> h i c n", i=4, c=2)
        S0 = 3 * T + 8 * N
        SLOTS = 21
        small = x2_flat[0:NH, S0:S0 + SLOTS * (N + 1)].rearrange("h (i n) -> h i n", i=SLOTS)
        S0 += SLOTS * (N + 1)
        small_i = x2_flat[0:NH, S0:S0 + 3 * (N + 1)].bitcast(I32).rearrange("h (i n) -> h i n", i=3)
        S0 += 3 * (N + 1)
        b1_nat = x2_flat[0:KC, S0:S0 + P]

        sC = sb("sC", [NH, N, 2])
        sX = sb("sX", [NH, N + 1])
        sAi = sb("sAi", [NH, N])
        zt = sb("zt", [P, 4, NH])
        D_row = sb("D_row", [LA, NH])

        logit = sb("logit", [P, NT, E])
        top_v = sb("top_v", [P, NT, 8])
        top_i = sb("top_i", [P, NT, 8], U32)
        top_f = sb("top_f", [P, NT, 2])
        gdiff = sb("gdiff", [P, NT])
        gexp = sb("gexp", [P, NT])
        gsum = sb("gsum", [P, NT])
        grec = sb("grec", [P, NT])
        gw = sb("gw", [P, NT, 2])
        onehot = sb("onehot", [P, NT, 2, E])
        gates = sb("gates", [P, NT, E])
        gated_h = w0_diag
        gh16 = w0_rows_sb[:, :].bitcast(F16).rearrange("p (c t n) -> p c t n", c=2, t=NT)
        conv_out = x2_sb[:, :, :, :].rearrange("p s h b -> p s (h b)")

        bank = [ctx.enter_context(nc.psum_tensor(f"bank{i}", [P, 512], F32)) for i in range(8)]

        full = [sem(f"psum_full{i}") for i in range(8)]
        free = [sem(f"psum_free{i}") for i in range(8)]
        unit = {}
        used = [0] * 8

        def add_unit(key, b):
            unit[key] = (b, used[b])
            used[b] += 1

        order = [("w1t", k) for k in range(KC)] + [("z", 0)] + [("l0", g) for g in range(NG0)]
        order += [("la", j) for j in range(NGA)] + [("w2t", k) for k in range(KC)]
        order += [("a2t", 0), ("wrt", 0), ("b2t", 0)]
        l1_order = [(m, n) for m in range(KC) for n in range(2)]
        for i, mn in enumerate(l1_order):
            if i == 4:
                order += [("k", 0), ("k", 1)]
            order.append(("l1", mn))
        for i, key in enumerate(order):
            add_unit(key, i % 8)
        for t in range(NT):
            if t % 2 == 0:
                add_unit(("aw", t // 2), t // 2)
        for t in range(NT):
            add_unit(("gt", t), 7)
            add_unit(("l2", t), 4 + t % 3)
        for t in range(NT):
            add_unit(("x3t", t), 2 + t % 2)
            add_unit(("conv", t), t % 2)

        def ps(key):
            return bank[unit[key][0]]

        def claim(eng, key):
            b, n = unit[key]
            if n:
                eng.wait_ge(free[b], n)

        def await_unit(eng, key):
            b, n = unit[key]
            eng.wait_ge(full[b], n + 1)

        def await_read(eng, key):
            b, n = unit[key]
            eng.wait_ge(free[b], n + 1)

        def full_of(key):
            return full[unit[key][0]]

        def free_of(key):
            return free[unit[key][0]]

        ids_in = sem("ids_in")
        cond_in = sem("cond_in")
        slot_in = sem("slot_in")
        x_in = [sem(f"x_in{g}") for g in range(NG0)]
        w1_in = sem("w1_in")
        w2_in = sem("w2_in")
        a2_in = sem("a2_in")
        b2_in = sem("b2_in")
        bias_ready = sem("bias_ready")
        s4_in = sem("s4_in")
        w0_got = sem("w0_got")
        la_got = sem("la_got")
        lb_got = sem("lb_got")
        w0_put = sem("w0_put")
        la_put = sem("la_put")
        lb_put = sem("lb_put")
        w0_in = sem("w0_in")
        la_in = sem("la_in")
        lb_in = sem("lb_in")
        consts = sem("consts")
        steps_ready = sem("steps_ready")
        pool_chain = sem("pool_chain")
        chain = sem("dve_chain")
        act_chain = sem("act_chain")
        eye_added1 = sem("eye_added1")
        eye_added2 = sem("eye_added2")
        w0_ready = sem("w0_ready")
        w1t_hi = sem("w1t_hi")
        w1t_ready = sem("w1t_ready")
        half_angle = sem("half_angle")
        half_trig = sem("half_trig")
        z_ready = sem("z_ready")
        x1_hi = sem("x1_hi")
        x1_ready = sem("x1_ready")
        la_hi = sem("la_hi")
        la_ready = sem("la_ready")
        lb_hi = sem("lb_hi")
        lb_ready = sem("lb_ready")
        lh_hi = sem("lh_hi")
        lh_ready = sem("lh_ready")
        decay_ready = sem("decay_ready")
        mag_ready = sem("mag_ready")
        angle_ready = sem("angle_ready")
        trig_ready = sem("trig_ready")
        pq_ready = sem("pq_ready")
        k_scaled = sem("k_scaled")
        k_ready = sem("k_ready")
        k_put = sem("k_put")
        zeros_put = sem("zeros_put")
        toep_in = [sem(f"toep_in{g}") for g in range(NT)]
        w2_hi = sem("w2_hi")
        w2_ready = sem("w2_ready")
        x2_hi = sem("x2_hi")
        x2_ready = sem("x2_ready")
        gap_ready = sem("gap_ready")
        gexp_ready = sem("gexp_ready")
        gt_hi = sem("gt_hi")
        gt_ready = sem("gt_ready")
        x3t_hi = sem("x3t_hi")
        x3t_ready = sem("x3t_ready")
        out_ready = sem("out_ready")
        out_put = [sem(f"out_put{i}") for i in range(4)]

        block = ctx.enter_context(nc.Block())
        kern_rows = kern_dram.ap()

        @block.sync
        def _(sp):
            sp.dma_start(gather_ids[:, 0:1], cond.rearrange("(b a) -> b a", a=1)).then_inc(cond_in, 16)
            sp.dma_start(gather_ids[:, 1:2], slot.rearrange("(b a) -> b a", a=1)).then_inc(slot_in, 16)
            sp.dma_start(w1_nat[:, :, :], W1.rearrange("(k p) i -> p k i", p=P)).then_inc(w1_in, 16)
            for g in range(NG0):
                sp.dma_start(x_sb[:, g, :], x[g * G0:(g + 1) * G0].rearrange("b c t -> (b c) t")).then_inc(x_in[g], 16)
            sp.wait_ge(w0_got, 16)
            sp.dma_start(w0_dram.ap(), w0_rows[:, :]).then_inc(w0_put, 16)
            sp.wait_ge(la_got, 16)
            sp.dma_start(la_dram.ap(), la_rows).then_inc(la_put, 16)
            sp.wait_ge(w0_put, 16)
            sp.dma_start(w0_blocks[:, :, :],
                         w0_dram.ap().rearrange("(g b) (c d) -> (b c) g d", b=G0, d=NH)).then_inc(w0_in, 16)
            sp.wait_ge(lb_got, 16)
            sp.dma_start(lb_dram.ap(), lb_rows).then_inc(lb_put, 16)
            sp.wait_ge(la_put, 16)
            sp.dma_start(la_sb[:, :, :], la_dram.ap().rearrange("b (p j) -> p b j", p=P)).then_inc(la_in, 16)
            sp.wait_ge(lb_put, 16)
            sp.dma_start(lb_sb[:, :, :],
                         lb_dram.ap().rearrange("(g b) (r o) -> (b r) g o", b=GA, o=T)).then_inc(lb_in, 16)
            for k in range(KC):
                await_unit(sp, ("w1t", k))
            sp.dma_start(w2_nat[:, :, :], W2.rearrange("(k p) i -> p k i", p=P)).then_inc(w2_in, 16)
            for k in range(KC):
                sp.dma_start(b2_nat[:, k], B2[:, k * P:(k + 1) * P, :].rearrange("e p r -> p e r")).then_inc(b2_in, 16)
            sp.wait_ge(k_ready, 1)
            sp.dma_start(kern_rows[:, 0:T].rearrange("(h c) (a b) -> a (h c) b", c=2, b=LB),
                         k16[:, :, :, :].rearrange("a h c b -> a (h c) b")).then_inc(k_put, 16)
            sp.wait_ge(k_put, 16)
            sp.wait_ge(zeros_put, 16)
            for g in range(NT):
                rows = 2 * HT
                src = bass.AP(kern_rows.tensor, g * rows * KPAD, [[1, P], [KPAD, rows], [1, T]])
                sp.dma_start(toep[:, g * HT:(g + 1) * HT, :, :].rearrange("p h c t -> p (h c) t"),
                             src).then_inc(toep_in[g], 16)
            for t in range(NT):
                sp.wait_ge(out_ready, t + 1)
                for h in range(HT):
                    sp.dma_start(out[:, t * HT + h, :], out_sb[h * NB:(h + 1) * NB, t % 4, :]).then_inc(out_put[t % 4], 16)
            for i in range(4):
                sp.wait_ge(out_put[i], 16 * HT * (NT // 4))

        @block.gpsimd
        def _(pool):
            pool.wait_ge(cond_in, 16)
            pool.indirect_dma_start(out=w0_rows[:, :], out_offset=None, in_=W0.rearrange("s c d -> s (c d)"),
                                    in_offset=bass.IndirectOffsetOnAxis(gather_ids[:, 0:1].bitcast(U32), 0)).then_inc(w0_got, 16)
            pool.wait_ge(slot_in, 16)
            pool.indirect_dma_start(out=la_rows, out_offset=None, in_=lora_A.rearrange("s i r -> s (i r)"),
                                    in_offset=bass.IndirectOffsetOnAxis(gather_ids[:, 1:2].bitcast(U32), 0)).then_inc(la_got, 16)
            pool.indirect_dma_start(out=lb_rows, out_offset=None, in_=lora_B.rearrange("s r o -> s (r o)"),
                                    in_offset=bass.IndirectOffsetOnAxis(gather_ids[:, 1:2].bitcast(U32), 0)).then_inc(lb_got, 16)

            count = [0]

            def link(ins):
                count[0] += 1
                ins.then_inc(pool_chain, 1)
                pool.wait_ge(pool_chain, count[0])

            link(nc.gpsimd.memset(ident[:, :], 0.0))
            nc.gpsimd.affine_select(out=ident[:, :], in_=ident[:, :], compare_op=ALU.not_equal, fill=1.0, base=0,
                                    pattern=[[-1, P]], channel_multiplier=1).then_inc(consts, 1)
            for mask, blocks, rows, value in ((w0_mask, G0, NH, 1.0), (lora_mask, GA, R, 2.0 / WS)):
                link(nc.gpsimd.memset(mask[:, :, :], value))
                link(nc.gpsimd.affine_select(out=mask[:, :, :], in_=mask[:, :, :], compare_op=ALU.is_ge, fill=0.0, base=0,
                                             pattern=[[-rows, blocks], [0, NH]], channel_multiplier=1))
                nc.gpsimd.affine_select(out=mask[:, :, :], in_=mask[:, :, :], compare_op=ALU.is_ge, fill=0.0,
                                        base=rows - 1, pattern=[[rows, blocks], [0, NH]],
                                        channel_multiplier=-1).then_inc(consts, 1)
            nc.gpsimd.iota(powers_i[:, 0:LB], pattern=[[-1, LB]], base=LB - 1, channel_multiplier=0).then_inc(steps_ready, 1)
            nc.gpsimd.iota(powers_i[:, LB:NL], pattern=[[-LB, LA]], base=T - LB, channel_multiplier=0).then_inc(steps_ready, 1)
            nc.gpsimd.iota(steps_i, pattern=[[1, T]], base=0, channel_multiplier=0).then_inc(steps_ready, 1)
            link(nc.gpsimd.memset(zeros16[:, :], 0.0))
            pool.dma_start(kern_rows[:, T:], zeros16[:, :]).then_inc(zeros_put, 16)

            pool.wait_ge(la_hi, 1)
            la_v = la_sb[:, :, :].rearrange("p b (k r) -> p k b r", k=KC)
            nc.gpsimd.tensor_tensor(la16[:, 1], la_v, la16[:, 0], ALU.subtract).then_inc(la_ready, 1)
            pool.wait_ge(lb_hi, 1)
            nc.gpsimd.tensor_tensor(lb16[:, 1], lb_sb[:, :, :], lb16[:, 0], ALU.subtract).then_inc(lb_ready, 1)
            for j in range(NGA):
                pool.wait_ge(lh_hi, j + 1)
                nc.gpsimd.tensor_tensor(lora_h16[:, 1, j, :], lora_h[:, j, :], lora_h16[:, 0, j, :],
                                        ALU.subtract).then_inc(lh_ready, 1)
            pool.wait_ge(z_ready, 1)
            await_read(pool, ("z", 0))
            pool.wait_ge(la_ready, 1)
            pool.wait_ge(lb_ready, 1)
            nc.gpsimd.tensor_tensor(tab_mag[:, :, :], zt[:, 0, :].unsqueeze(2).to_broadcast([P, NH, NL]),
                                    powers[:, :].unsqueeze(1).to_broadcast([P, NH, NL]), ALU.mult).then_inc(decay_ready, 1)
            for i, (m, n) in enumerate(l1_order):
                pool.wait_ge(x2_hi, i + 1)
                dst = x2t16[:, :, m, :, n * (NB // 2):(n + 1) * (NB // 2)]
                nc.gpsimd.tensor_tensor(dst[:, 1], x2_sb[:, i % 2], dst[:, 0], ALU.subtract).then_inc(x2_ready, 1)
            for t in range(NT):
                await_read(pool, ("conv", t))
                if t >= 4:
                    pool.wait_ge(out_put[t % 4], 16 * HT * (t // 4))
                nc.gpsimd.tensor_tensor(out_sb[:, t % 4, :], conv_out[:, t % 2, :], x_sb[:, t, :],
                                        ALU.add).then_inc(out_ready, 1)

        @block.scalar
        def _(act):
            act.dma_start(sX[:, 0:N], log_A_real).then_inc(s4_in, 16)
            act.dma_start(sX[:, N:N + 1], log_dt.rearrange("(h a) -> h a", a=1)).then_inc(s4_in, 16)
            act.dma_start(sAi[:, :], A_imag).then_inc(s4_in, 16)
            act.dma_start(sC[:, :, :], C).then_inc(s4_in, 16)
            act.dma_start(D_row[:, :], bass.AP(D.tensor, 0, [[0, LA], [1, NH]])).then_inc(s4_in, 16)
            for q in range(HT):
                act.dma_start(ids_i[q * NB:(q + 1) * NB, 0:1], lang.rearrange("(b a) -> b a", a=1)).then_inc(ids_in, 16)
                act.dma_start(ids_i[q * NB:(q + 1) * NB, 1:2], length.rearrange("(b a) -> b a", a=1)).then_inc(ids_in, 16)
            act.dma_start(b1_nat, b1.rearrange("(k p) -> k p", p=P)).then_inc(a2_in, 16)
            act.dma_start(a2_nat[:, :], A2.rearrange("e r i -> (e r) i")).then_inc(a2_in, 16)
            act.dma_start(wr_nat[:, :], Wr).then_inc(a2_in, 16)

            for k in range(KC):
                await_unit(act, ("w1t", k))
                nc.scalar.activation(w1t[:, 0, k, :], ps(("w1t", k))[:, :], ACT.Copy, scale=WS).then_inc(w1t_hi, 1)
            act.wait_ge(half_angle, 2)
            nc.scalar.activation(small[:, 10, 0:N], small[:, 8, 0:N], ACT.Sin).then_inc(half_trig, 1)
            nc.scalar.activation(small[:, 11, 0:N], small[:, 9, 0:N], ACT.Sin).then_inc(half_trig, 1)
            for g in range(NG0):
                await_unit(act, ("l0", g))
                nc.scalar.activation(xt16[:, 0, :, g * P:(g + 1) * P],
                                     ps(("l0", g))[:, :].rearrange("p (k n) -> p k n", k=KC), ACT.Copy).then_inc(x1_hi, 1)
            act.wait_ge(la_in, 16)
            nc.scalar.activation(la_sb[:, :, :], la_sb[:, :, :], ACT.Copy, scale=WS).then_inc(act_chain, 1)
            act.wait_ge(lb_in, 16)
            nc.scalar.activation(lb_sb[:, :, :], lb_sb[:, :, :], ACT.Copy, scale=WS).then_inc(act_chain, 1)
            act.wait_ge(act_chain, 1)
            nc.scalar.activation(la16[:, 0], la_sb[:, :, :].rearrange("p b (k r) -> p k b r", k=KC),
                                 ACT.Copy).then_inc(la_hi, 1)
            act.wait_ge(act_chain, 2)
            nc.scalar.activation(lb16[:, 0], lb_sb[:, :, :], ACT.Copy).then_inc(lb_hi, 1)
            for j in range(NGA):
                await_read(act, ("la", j))
                nc.scalar.activation(lora_h16[:, 0, j, :], lora_h[:, j, :], ACT.Copy).then_inc(lh_hi, 1)
            for k in range(KC):
                await_unit(act, ("w2t", k))
                nc.scalar.activation(w2t[:, 0, k, :], ps(("w2t", k))[:, :], ACT.Copy, scale=WS).then_inc(w2_hi, 1)
            await_unit(act, ("a2t", 0))
            nc.scalar.activation(awt[:, 0, :, 0:P], ps(("a2t", 0))[:, :].rearrange("p (k n) -> p k n", k=KC),
                                 ACT.Copy, scale=WS).then_inc(w2_hi, 1)
            await_unit(act, ("wrt", 0))
            nc.scalar.activation(awt[:, 0, :, P:AW], ps(("wrt", 0))[:, 0:KC * E].rearrange("p (k n) -> p k n", k=KC),
                                 ACT.Copy, scale=WS).then_inc(w2_hi, 1)
            await_unit(act, ("b2t", 0))
            nc.scalar.activation(b2t[:, 0, :], ps(("b2t", 0))[:, :], ACT.Copy, scale=WS).then_inc(w2_hi, 1)
            act.wait_ge(decay_ready, 1)
            nc.scalar.activation(tab_mag[:, :, :], tab_mag[:, :, :], ACT.Exp).then_inc(mag_ready, 1)
            act.wait_ge(angle_ready, 2)
            nc.scalar.activation(trig_b[0:N], tab_abs[0:N, :, 0:LB], ACT.Sin).then_inc(trig_ready, 1)
            nc.scalar.activation(trig_b[N:P], tab_th[N:P, :, 0:LB], ACT.Sin).then_inc(trig_ready, 1)
            nc.scalar.activation(cos_a[:, :, :], tab_abs[:, :, LB:NL], ACT.Sin).then_inc(trig_ready, 1)
            nc.scalar.activation(sin_a[:, :, :], tab_th[:, :, LB:NL], ACT.Sin).then_inc(trig_ready, 1)
            act.wait_ge(bias_ready, 1)
            for i, (m, n) in enumerate(l1_order):
                await_unit(act, ("l1", (m, n)))
                if i >= 2:
                    act.wait_ge(x2_ready, i - 1)
                nc.scalar.activation(x2_sb[:, i % 2], ps(("l1", (m, n)))[:, :].rearrange("p (b h) -> p h b", h=NH),
                                     ACT.Identity, bias=bias_sb[:, m:m + 1],
                                     scale=1.0 / WS).then_inc(free_of(("l1", (m, n))), 1)
                await_read(act, ("l1", (m, n)))
                nc.scalar.activation(x2t16[:, 0, m, :, n * (NB // 2):(n + 1) * (NB // 2)], x2_sb[:, i % 2],
                                     ACT.Copy).then_inc(x2_hi, 1)
            for s in range(2):
                act.wait_ge(gap_ready, s + 1)
                nc.scalar.activation(gexp[:, s * 4:s * 4 + 4], gdiff[:, s * 4:s * 4 + 4], ACT.Exp).then_inc(gexp_ready, 1)

            act.wait_ge(k_put, 16)

            def gh_high(t):
                await_unit(act, ("gt", t))
                nc.scalar.activation(gh16[:, 0, t, :], ps(("gt", t))[:, 0:P], ACT.Copy).then_inc(gt_hi, 1)

            def x3_sum(t):
                await_unit(act, ("l2", t))
                nc.scalar.activation(x_sb[:, t, :], ps(("l2", t))[:, :], ACT.Copy, scale=1.0 / WS).then_inc(free_of(("l2", t)), 1)

            def x3t_high(t):
                await_unit(act, ("x3t", t))
                nc.scalar.activation(xt16[:, 0, :, t * P:(t + 1) * P],
                                     ps(("x3t", t))[:, :].rearrange("p (k n) -> p k n", k=KC), ACT.Copy).then_inc(x3t_hi, 1)

            for i in range(NT + 2):
                if i < NT:
                    gh_high(i)
                if 1 <= i <= NT:
                    x3_sum(i - 1)
                if i >= 2:
                    x3t_high(i - 2)

        @block.vector
        def _(dve):
            count = [0]
            V = nc.vector

            def link(ins):
                count[0] += 1
                ins.then_inc(chain, 1)
                dve.wait_ge(chain, count[0])

            def exp_parts(src, w, slot0, islot):
                ki, p2 = small_i[:, islot, 0:w], small_i[:, islot + 1, 0:w]
                r, q = small[:, slot0, 0:w], small[:, slot0 + 1, 0:w]
                link(V.tensor_scalar(ki, src, 1.0 / math.log(2.0), None, ALU.mult))
                link(V.scalar_tensor_tensor(r, ki, -LN2_HI, src, ALU.mult, ALU.add))
                link(V.scalar_tensor_tensor(r, ki, -LN2_LO, r, ALU.mult, ALU.add))
                link(V.tensor_scalar(q, r, 1.0 / math.factorial(EXP_TERMS), None, ALU.mult))
                for n in range(EXP_TERMS - 1, 0, -1):
                    link(V.scalar_tensor_tensor(q, q, 1.0 / math.factorial(n), r, ALU.add, ALU.mult))
                link(V.tensor_scalar(p2, ki, 127.0, 0.0, ALU.add, ALU.max))
                link(V.tensor_scalar(p2, p2, 23, None, ALU.logical_shift_left))
                return q, p2.bitcast(F32)

            def reduce_angle(th, ki):
                link(V.tensor_scalar(ki, th, 1.0 / TWO_PI, None, ALU.mult))
                for part in (PI_HI, PI_MID, PI_LO):
                    link(V.scalar_tensor_tensor(th, ki, -part, th, ALU.mult, ALU.add))
                link(V.tensor_scalar(th, th, PI_DOWN, -PI_DOWN, ALU.min, ALU.max))

            dve.wait_ge(s4_in, 16 * 5)
            q, p2 = exp_parts(sX[:, :], N + 1, 0, 0)
            rates = small[:, 2, :]
            link(V.scalar_tensor_tensor(rates, q, 1.0, p2, ALU.add, ALU.mult))
            rate, dt = small[:, 2, 0:N], small[:, 2, N:N + 1]
            dre, dim = small[:, 3, 0:N], small[:, 4, 0:N]
            link(V.tensor_scalar(dre, rate, dt, -1.0, ALU.mult, ALU.mult))
            link(V.tensor_scalar(dim, sAi[:, :], dt, None, ALU.mult))
            ha, hc = small[:, 8, 0:N], small[:, 9, 0:N]
            link(V.tensor_scalar(ha, dim, 0.5, None, ALU.mult))
            reduce_angle(ha, small_i[:, 2, 0:N])
            link(V.tensor_scalar(hc, ha, -1.0, None, ALU.mult))
            link(V.tensor_tensor(hc, hc, ha, ALU.min))
            V.tensor_scalar(hc, hc, math.pi / 2, None, ALU.add).then_inc(half_angle, 2)
            dve.wait_ge(w1_in, 16)
            dve.wait_ge(consts, 3)
            for k in range(KC):
                d = w1_nat[:, k, k * P:(k + 1) * P]
                V.tensor_tensor(d, d, ident[:, :], ALU.add).then_inc(eye_added1, 1)
            q, p2 = exp_parts(dre, N, 5, 0)
            em1, e1 = small[:, 7, 0:N], small[:, 12, 0:N]
            link(V.tensor_scalar(e1, p2, -1.0, None, ALU.add))
            link(V.tensor_tensor(em1, q, p2, ALU.mult))
            link(V.tensor_tensor(em1, em1, e1, ALU.add))
            link(V.tensor_scalar(e1, em1, 1.0, None, ALU.add))
            dve.wait_ge(half_trig, 2)
            sn, cs = small[:, 10, 0:N], small[:, 11, 0:N]
            t0, t1, t2, er, ei = (small[:, i, 0:N] for i in (13, 14, 15, 16, 17))
            fr, fi, inv = (small[:, i, 0:N] for i in (18, 19, 20))
            link(V.tensor_tensor(t0, sn, sn, ALU.mult))
            link(V.tensor_tensor(t0, t0, e1, ALU.mult))
            link(V.scalar_tensor_tensor(er, t0, -2.0, em1, ALU.mult, ALU.add))
            link(V.tensor_tensor(t1, sn, cs, ALU.mult))
            link(V.scalar_tensor_tensor(ei, t1, 2.0, e1, ALU.mult, ALU.mult))
            link(V.tensor_tensor(t0, rate, rate, ALU.mult))
            link(V.tensor_tensor(t1, sAi[:, :], sAi[:, :], ALU.mult))
            link(V.tensor_tensor(t0, t0, t1, ALU.add))
            link(V.reciprocal(inv, t0))
            link(V.scalar_tensor_tensor(t0, er, -1.0, rate, ALU.mult, ALU.mult))
            link(V.tensor_tensor(t1, ei, sAi[:, :], ALU.mult))
            link(V.tensor_tensor(fr, t0, t1, ALU.add))
            link(V.scalar_tensor_tensor(t0, ei, -1.0, rate, ALU.mult, ALU.mult))
            link(V.tensor_tensor(t1, er, sAi[:, :], ALU.mult))
            link(V.tensor_tensor(fi, t0, t1, ALU.subtract))
            link(V.scalar_tensor_tensor(fr, fr, 2.0, inv, ALU.mult, ALU.mult))
            link(V.scalar_tensor_tensor(fi, fi, 2.0, inv, ALU.mult, ALU.mult))
            cr, ci = sC[:, :, 0], sC[:, :, 1]
            link(V.tensor_tensor(t0, cr, fr, ALU.mult))
            link(V.tensor_tensor(t1, ci, fi, ALU.mult))
            link(V.tensor_tensor(zcat[:, 2, 0, :], t0, t1, ALU.subtract))
            link(V.tensor_tensor(t2, cr, fi, ALU.mult))
            link(V.tensor_tensor(t0, ci, fr, ALU.mult))
            link(V.scalar_tensor_tensor(zcat[:, 2, 1, :], t2, -1.0, t0, ALU.mult, ALU.subtract))
            link(V.tensor_copy(zcat[:, 3, 0, :], zcat[:, 2, 1, :]))
            link(V.tensor_scalar(zcat[:, 3, 1, :], zcat[:, 2, 0, :], -1.0, None, ALU.mult))
            for half in range(2):
                link(V.tensor_copy(zcat[:, 0, half, :], dre))
                link(V.tensor_copy(zcat[:, 1, half, :], dim))
            dve.wait_ge(steps_ready, 3)
            V.tensor_copy(powers[:, :], powers_i[:, :]).then_inc(z_ready, 1)
            dve.wait_ge(w0_in, 16)
            diag4 = w0_diag[:, :, :].rearrange("p g (b d) -> p g b d", b=G0)
            link(V.tensor_tensor(diag4, w0_blocks[:, :, :].unsqueeze(2).to_broadcast([P, NG0, G0, NH]),
                                 w0_mask[:, :, :].unsqueeze(1).to_broadcast([P, NG0, G0, NH]), ALU.mult))
            V.tensor_tensor(w0_diag[:, :, :], w0_diag[:, :, :],
                            ident[:, :].unsqueeze(1).to_broadcast([P, NG0, P]), ALU.add).then_inc(w0_ready, 1)
            for k in range(KC):
                dve.wait_ge(w1t_hi, k + 1)
                V.scalar_tensor_tensor(w1t[:, 1, k, :], ps(("w1t", k))[:, :], WS, w1t[:, 0, k, :],
                                       ALU.mult, ALU.subtract).then_inc(free_of(("w1t", k)), 1)
            await_unit(dve, ("z", 0))
            V.tensor_copy(zt[:, :, :].rearrange("p a h -> p (a h)"), ps(("z", 0))[:, 0:4 * NH]).then_inc(free_of(("z", 0)), 1)
            for g in range(NG0):
                dve.wait_ge(x1_hi, g + 1)
                V.tensor_tensor(xt16[:, 1, :, g * P:(g + 1) * P], ps(("l0", g))[:, :].rearrange("p (k n) -> p k n", k=KC),
                                xt16[:, 0, :, g * P:(g + 1) * P], ALU.subtract).then_inc(free_of(("l0", g)), 1)
            for j in range(NGA):
                await_unit(dve, ("la", j))
                V.tensor_tensor(lora_h[:, j, :], ps(("la", j))[:, 0:TA],
                                lora_mask[:, :, :].rearrange("p b h -> p (b h)"), ALU.mult).then_inc(free_of(("la", j)), 1)
            dve.wait_ge(ids_in, 16 * 2 * HT)
            link(V.tensor_copy(ids[:, :], ids_i[:, :]))
            link(V.tensor_copy(steps[:, :], steps_i))
            V.tensor_scalar(conv_mask[:, :], steps[:, :], ids[:, 1:2], 1.0 / WS, ALU.is_lt, ALU.mult)
            V.tensor_scalar(lang_bias[:, :], steps[:, 0:E], ids[:, 0:1], 5.0, ALU.is_equal, ALU.mult)
            dve.wait_ge(w2_in, 16)
            for k in range(KC):
                d = w2_nat[:, k, k * P:(k + 1) * P]
                V.tensor_tensor(d, d, ident[:, :], ALU.add).then_inc(eye_added2, 1)
            for k in range(KC):
                dve.wait_ge(w2_hi, k + 1)
                V.scalar_tensor_tensor(w2t[:, 1, k, :], ps(("w2t", k))[:, :], WS, w2t[:, 0, k, :],
                                       ALU.mult, ALU.subtract).then_inc(free_of(("w2t", k)), 1)
            dve.wait_ge(w2_hi, KC + 1)
            V.scalar_tensor_tensor(awt[:, 1, :, 0:P], ps(("a2t", 0))[:, :].rearrange("p (k n) -> p k n", k=KC), WS,
                                   awt[:, 0, :, 0:P], ALU.mult, ALU.subtract).then_inc(free_of(("a2t", 0)), 1)
            dve.wait_ge(w2_hi, KC + 2)
            V.tensor_copy(bias_sb[:, :], ps(("wrt", 0))[:, KC * E:KC * E + KC]).then_inc(bias_ready, 1)
            V.scalar_tensor_tensor(awt[:, 1, :, P:AW], ps(("wrt", 0))[:, 0:KC * E].rearrange("p (k n) -> p k n", k=KC), WS,
                                   awt[:, 0, :, P:AW], ALU.mult, ALU.subtract).then_inc(free_of(("wrt", 0)), 1)
            dve.wait_ge(w2_hi, KC + 3)
            V.scalar_tensor_tensor(b2t[:, 1, :], ps(("b2t", 0))[:, :], WS, b2t[:, 0, :],
                                   ALU.mult, ALU.subtract).then_inc(free_of(("b2t", 0)), 1)
            dve.wait_ge(lb_ready, 1)
            link(V.tensor_tensor(tab_th[:, :, :], zt[:, 1, :].unsqueeze(2).to_broadcast([P, NH, NL]),
                                 powers[:, :].unsqueeze(1).to_broadcast([P, NH, NL]), ALU.mult))
            reduce_angle(tab_th[:, :, :], tab_ki[:, :, :])
            link(V.tensor_scalar(tab_abs[:, :, :], tab_th[:, :, :], -1.0, None, ALU.mult))
            link(V.tensor_tensor(tab_abs[:, :, :], tab_abs[:, :, :], tab_th[:, :, :], ALU.min))
            V.tensor_scalar(tab_abs[:, :, :], tab_abs[:, :, :], math.pi / 2, None, ALU.add).then_inc(angle_ready, 2)
            dve.wait_ge(mag_ready, 1)
            dve.wait_ge(trig_ready, 4)
            V.tensor_tensor(trig_b[:, :, :], trig_b[:, :, :], tab_mag[:, :, 0:LB], ALU.mult).then_inc(pq_ready, 1)
            link(V.tensor_tensor(cos_a[:, :, :], cos_a[:, :, :],
                                 zt[:, 2, :].unsqueeze(2).to_broadcast([P, NH, LA]), ALU.mult))
            link(V.tensor_tensor(sin_a[:, :, :], sin_a[:, :, :],
                                 zt[:, 3, :].unsqueeze(2).to_broadcast([P, NH, LA]), ALU.mult))
            link(V.tensor_tensor(cos_a[:, :, :], cos_a[:, :, :], sin_a[:, :, :], ALU.add))
            V.tensor_tensor(cos_a[:, :, :], cos_a[:, :, :], tab_mag[:, :, LB:NL], ALU.mult).then_inc(pq_ready, 1)
            HH = NH // 2
            for s in range(2):
                await_unit(dve, ("k", s))
                V.tensor_scalar(k64[:, s * HH:(s + 1) * HH, :].rearrange("a h b -> a (h b)"), ps(("k", s))[0:LA, :], WS,
                                None, ALU.mult).then_inc(free_of(("k", s)), 1)
            await_read(dve, ("k", 0))
            await_read(dve, ("k", 1))
            link(V.tensor_scalar(D_row[:, :], D_row[:, :], ident[0:LA, LA - 1:LA], WS, ALU.mult, ALU.mult))
            link(V.tensor_tensor(k64[:, :, LB - 1], k64[:, :, LB - 1], D_row[:, :], ALU.add))
            link(V.tensor_copy(k16[:, :, 0, :], k64[:, :, :]))
            V.tensor_tensor(k16[:, :, 1, :], k64[:, :, :], k16[:, :, 0, :], ALU.subtract).then_inc(k_ready, 1)

            def logits(t):
                await_unit(dve, ("aw", t // 2))
                at = (t % 2) * AW
                link(V.scalar_tensor_tensor(logit[:, t, :], ps(("aw", t // 2))[:, at + P:at + AW], 1.0 / WS,
                                            lang_bias[:, :], ALU.mult, ALU.add))
                link(V.max(top_v[:, t, :], logit[:, t, :]))
                link(V.max_index(top_i[:, t, :], top_v[:, t, :], logit[:, t, :]))

            for s in range(2):
                S = slice(s * 4, s * 4 + 4)
                for t in range(s * 4, s * 4 + 4):
                    logits(t)
                V.tensor_tensor(gdiff[:, S], top_v[:, S, 1], top_v[:, S, 0], ALU.subtract).then_inc(gap_ready, 1)
                link(V.tensor_copy(top_f[:, S, :], top_i[:, S, 0:2]))
                link(V.tensor_tensor(onehot[:, S], steps[:, 0:E].unsqueeze(1).unsqueeze(1).to_broadcast([P, 4, 2, E]),
                                     top_f[:, S, :].unsqueeze(3).to_broadcast([P, 4, 2, E]), ALU.is_equal))
                dve.wait_ge(gexp_ready, s + 1)
                link(V.tensor_scalar(gsum[:, S], gexp[:, S], 1.0, None, ALU.add))
                link(V.reciprocal(grec[:, S], gsum[:, S]))
                link(V.tensor_scalar(gw[:, S, 0], grec[:, S], 2.0 / WS, None, ALU.mult))
                link(V.tensor_tensor(gw[:, S, 1], gw[:, S, 0], gexp[:, S], ALU.mult))
                link(V.tensor_tensor(onehot[:, S], onehot[:, S], gw[:, S, :].unsqueeze(3).to_broadcast([P, 4, 2, E]), ALU.mult))
                link(V.tensor_tensor(gates[:, S, :], onehot[:, S, 0, :], onehot[:, S, 1, :], ALU.add))
                for t in range(s * 4, s * 4 + 4):
                    at = (t % 2) * AW
                    ins = V.tensor_tensor(gated_h[:, t, :].rearrange("p (e r) -> p e r", e=E),
                                          ps(("aw", t // 2))[:, at:at + P].rearrange("p (e r) -> p e r", e=E),
                                          gates[:, t, :].unsqueeze(2).to_broadcast([P, E, R]), ALU.mult)
                    if t % 2 == 1:
                        ins.then_inc(free_of(("aw", t // 2)), 1)

            def gh_low(t):
                dve.wait_ge(gt_hi, t + 1)
                V.tensor_tensor(gh16[:, 1, t, :], ps(("gt", t))[:, 0:P], gh16[:, 0, t, :],
                                ALU.subtract).then_inc(free_of(("gt", t)), 1)

            def x3t_low(t):
                dve.wait_ge(x3t_hi, t + 1)
                V.tensor_tensor(xt16[:, 1, :, t * P:(t + 1) * P], ps(("x3t", t))[:, :].rearrange("p (k n) -> p k n", k=KC),
                                xt16[:, 0, :, t * P:(t + 1) * P], ALU.subtract).then_inc(free_of(("x3t", t)), 1)

            def mask_conv(t):
                await_unit(dve, ("conv", t))
                if t >= 2:
                    dve.wait_ge(out_ready, t - 1)
                V.tensor_tensor(conv_out[:, t % 2, :], ps(("conv", t))[:, T - 1::-1], conv_mask[:, :],
                                ALU.mult).then_inc(free_of(("conv", t)), 1)

            for i in range(NT + 4):
                if i < NT:
                    gh_low(i)
                if 2 <= i < NT + 2:
                    x3t_low(i - 2)
                if i >= 4:
                    mask_conv(i - 4)

        @block.tensor
        def _(pe):
            mm = nc.tensor.matmul

            def transposes(key, sources, width, rows=P):
                claim(pe, key)
                for i, src in enumerate(sources):
                    last = nc.tensor.transpose(ps(key)[:, i * width:(i + 1) * width], src, ident[0:rows, 0:rows])
                last.then_inc(full_of(key), 1)

            pe.wait_ge(eye_added1, KC)
            for k in range(KC):
                transposes(("w1t", k), [w1_nat[:, m, k:T:KC] for m in range(KC)], P)
            pe.wait_ge(z_ready, 1)
            transposes(("z", 0), [zcat[:, i].rearrange("h c n -> h (c n)") for i in range(4)], NH, NH)
            pe.wait_ge(w0_ready, 1)
            for g in range(NG0):
                pe.wait_ge(x_in[g], 16)
                claim(pe, ("l0", g))
                for k in range(KC):
                    last = mm(ps(("l0", g))[:, k * P:(k + 1) * P], x_sb[:, g, k:T:KC], w0_diag[:, g, :],
                              start=True, stop=True)
                last.then_inc(full_of(("l0", g)), 1)

            def product(dst, pairs, first=True, final=True):
                n = len(pairs) * len(PARTS_USED)
                i = 0
                for lhs, rhs in pairs:
                    for a, b in PARTS_USED:
                        last = mm(dst, lhs(a), rhs(b), start=first and i == 0, stop=final and i == n - 1)
                        i += 1
                return last

            pe.wait_ge(la_ready, 1)
            for j in range(NGA):
                claim(pe, ("la", j))
                for g in range(2 * j, 2 * j + 2):
                    await_read(pe, ("l0", g))
                pairs = [(lambda a, k=k: la16[:, a, k, j * GA:(j + 1) * GA, :].rearrange("p b r -> p (b r)"),
                          lambda b, k=k: xt16[:, b, k, j * TA:(j + 1) * TA]) for k in range(KC)]
                product(ps(("la", j))[:, 0:TA], pairs).then_inc(full_of(("la", j)), 1)
            pe.wait_ge(eye_added2, KC)
            for k in range(KC):
                transposes(("w2t", k), [w2_nat[:, m, k * P:(k + 1) * P] for m in range(KC)], P)
            pe.wait_ge(a2_in, 48)
            transposes(("a2t", 0), [a2_nat[:, k * P:(k + 1) * P] for k in range(KC)], P)
            claim(pe, ("wrt", 0))
            nc.tensor.transpose(ps(("wrt", 0))[:, KC * E:KC * E + KC], b1_nat, ident[0:KC, 0:KC])
            transposes(("wrt", 0), [wr_nat[:, k * P:(k + 1) * P] for k in range(KC)], E, E)
            pe.wait_ge(b2_in, 16 * KC)
            transposes(("b2t", 0), [b2_nat[:, k].rearrange("p e r -> p (e r)") for k in range(KC)], P)
            for k in range(KC):
                await_read(pe, ("w1t", k))
            for g in range(NG0):
                await_read(pe, ("l0", g))
            pe.wait_ge(lh_ready, NGA)
            pe.wait_ge(lb_ready, 1)
            for i, (m, n) in enumerate(l1_order):
                if i == 4:
                    pe.wait_ge(pq_ready, 2)
                    for s in range(2):
                        claim(pe, ("k", s))
                        for h in range(NH // 2):
                            hh = s * (NH // 2) + h
                            last = mm(ps(("k", s))[0:LA, h * LB:(h + 1) * LB], cos_a[:, hh, :], trig_b[:, hh, :],
                                      start=True, stop=True)
                        last.then_inc(full_of(("k", s)), 1)
                key = ("l1", (m, n))
                claim(pe, key)
                M = slice(m * P, (m + 1) * P)
                pairs = [(lambda a, k=k: w1t[:, a, k, M], lambda b, k=k: xt16[:, b, k, n * HALF:(n + 1) * HALF])
                         for k in range(KC)]
                product(ps(key)[:, :], pairs, final=False)
                per = HALF // TA
                for j in range(n * per, (n + 1) * per):
                    c = (j - n * per) * TA
                    pairs = [(lambda a: lb16[:, a, j, M], lambda b: lora_h16[:, b, j, :])]
                    last = product(ps(key)[:, c:c + TA], pairs, first=False, final=(j == (n + 1) * per - 1))
                last.then_inc(full_of(key), 1)
            for t in range(NT):
                key = ("aw", t // 2)
                if t % 2 == 0:
                    claim(pe, key)
                at = (t % 2) * AW
                for k in range(KC):
                    if t == 0:
                        pe.wait_ge(x2_ready, 2 * (k + 1))
                    lhs = lambda a, k=k: x2t16[:, a, k, t * HT:(t + 1) * HT, :].rearrange("p h b -> p (h b)")
                    last = product(ps(key)[:, at:at + AW], [(lhs, lambda b, k=k: awt[:, b, k, :])],
                                   first=(k == 0), final=(k == KC - 1))
                if t % 2 == 1:
                    last.then_inc(full_of(key), 1)

            def main2(t):
                claim(pe, ("gt", t))
                await_read(pe, ("aw", t // 2))
                nc.tensor.transpose(ps(("gt", t))[:, 0:P], gated_h[:, t, :], ident[:, :]).then_inc(full_of(("gt", t)), 1)
                key = ("l2", t)
                claim(pe, key)
                pairs = [(lambda a, k=k: x2t16[:, a, k, t * HT:(t + 1) * HT, :].rearrange("p h b -> p (h b)"),
                          lambda b, k=k: w2t[:, b, k, :]) for k in range(KC)]
                product(ps(key)[:, :], pairs, final=False)
                await_read(pe, ("gt", t))
                product(ps(key)[:, :], [(lambda a: gh16[:, a, t, :], lambda b: b2t[:, b, :])],
                        first=False).then_inc(full_of(key), 1)

            def turn3(t):
                await_read(pe, ("l2", t))
                transposes(("x3t", t), [x_sb[:, t, k * P:(k + 1) * P] for k in range(KC)], P)

            def conv(t):
                key = ("conv", t)
                claim(pe, key)
                await_read(pe, ("x3t", t))
                pe.wait_ge(toep_in[t], 16)
                for k in range(KC):
                    for n, (a, b) in enumerate(PARTS_USED):
                        for h in range(HT):
                            rows = slice(h * NB, (h + 1) * NB)
                            last = mm(ps(key)[rows, 0:T - k * P], xt16[:, a, k, t * P + h * NB:t * P + (h + 1) * NB],
                                      toep[:, t * HT + h, b, k * P:T], start=(k == 0 and n == 0),
                                      stop=(k == KC - 1 and n == 2))
                last.then_inc(full_of(key), 1)

            for i in range(NT + 2):
                if i < NT:
                    main2(i)
                if 1 <= i <= NT:
                    turn3(i - 1)
                if i >= 2:
                    conv(i - 2)


_INS = ['x', 'itok_B_0_15', 'itok_B_0_23', 'itok_B_0_7', 'itok_B_8_3872', 'L0_cond_weights', 'L1_cond_W', 'L1_cond_b',
        'L1_cond_lora_As', 'L1_cond_lora_Bs', 'L2_cond_W', 'L2_cond_Wr', 'L2_cond_A', 'L2_cond_B', 'L3_cond_log_dt',
        'L3_cond_C', 'L3_cond_log_A_real', 'L3_cond_A_imag', 'L3_cond_D']


def kernel(**inputs):
    import numpy as _np
    import concourse.bacc as _bacc
    from concourse import mybir as _mybir
    from concourse.bass_utils import run_bass_kernel_spmd as _run

    nc = _bacc.Bacc("TRN2", target_bir_lowering=False, num_devices=1)
    arrays, args = {}, []
    for name in _INS:
        a = _np.ascontiguousarray(inputs[name])
        arrays[f"in_{name}_dram"] = a
        args.append(nc.dram_tensor(f"in_{name}_dram", a.shape, _mybir.dt.from_np(a.dtype), kind="ExternalInput").ap())
    shape = arrays["in_x_dram"].shape
    args.append(nc.dram_tensor("out_0_dram", shape, _mybir.dt.float32, kind="ExternalOutput").ap())
    cond_resid_kernel(nc, *args)
    r = _run(nc, [arrays], core_ids=[0])
    return r.results[0]["out_0_dram"]
```

```python
import math
from contextlib import ExitStack

import numpy as np
import concourse.bass as bass
from concourse import mybir

F32 = mybir.dt.float32
F16 = mybir.dt.float16
I32 = mybir.dt.int32
U32 = mybir.dt.uint32
ALU = mybir.AluOpType
ACT = mybir.ActivationFunctionType

P = 128
GATHER = 8
WS = 64.0
PARTS_USED = [(0, 0), (1, 0), (0, 1)]

TWO_PI = 2.0 * math.pi
PI_DOWN = 3.1415925


def cut(value, bits):
    m, e = math.frexp(value)
    return math.ldexp(math.floor(math.ldexp(m, bits)), e - bits)


PI_HI = cut(TWO_PI, 12)
PI_LO = TWO_PI - PI_HI
LN2_HI = cut(math.log(2.0), 12)
LN2_LO = math.log(2.0) - LN2_HI
EXP_TERMS = 7


def cond_resid_kernel(nc, x, cond, slot, lang, length, W0, W1, b1, lora_A, lora_B,
                      W2, Wr, A2, B2, log_dt, C, log_A_real, A_imag, D, out):
    NB, NH, T = x.shape
    KC = T // P
    R = lora_A.shape[2]
    E = Wr.shape[0]
    N = A_imag.shape[1]
    NTOK = NB * NH
    G0 = P // NH
    NG0 = NB // G0
    GA = P // R
    NGA = NB // GA
    TA = GA * NH
    NT = NTOK // P
    HT = P // NB
    HALF = NTOK // 2
    LB = 32
    LA = T // LB
    NL = LB + LA
    NTAB = NH * NL
    AW = E * R + E
    KPAD = T + P
    assert 2 * N == P and E * R == P and T == KC * P and E == 8

    kern_dram = nc.dram_tensor("conv_kernels", [NH * 2, KPAD], F16)

    with ExitStack() as ctx:
        def sb(name, shape, dt=F32):
            return ctx.enter_context(nc.sbuf_tensor(name, shape, dt))

        def sem(name):
            return ctx.enter_context(nc.semaphore(name))

        ident = sb("ident", [P, P])
        w0_mask = sb("w0_mask", [P, G0, NH])
        lora_mask = sb("lora_mask", [P, GA, NH])
        steps = sb("steps", [P, T])
        powers_i = sb("powers_i", [P, NL], I32)
        powers = sb("powers", [P, NL])
        ids_i = sb("ids_i", [NB, 2], I32)
        ids = sb("ids", [P, 2])
        cond_bc = sb("cond_bc", [P, NB], I32)
        slot_bc = sb("slot_bc", [P, NB], I32)
        cond_own = sb("cond_own", [P, NG0, G0])
        slot_own = sb("slot_own", [P, NGA, GA])
        cond_sum = sb("cond_sum", [P, NG0])
        slot_sum = sb("slot_sum", [P, NGA])
        lane = sb("lane", [P, 1], I32)
        lane_mod = sb("lane_mod", [P, 2], I32)
        w0_index = sb("w0_index", [P, NG0], U32)
        lb_index = sb("lb_index", [P, NGA], U32)
        half_pi = sb("half_pi", [P, 1])
        conv_mask = sb("conv_mask", [P, T])
        steps_i = conv_mask[:, :].bitcast(I32)
        lang_bias = sb("lang_bias", [P, E])
        bias_sb = sb("bias_sb", [P, KC])

        x_sb = sb("x_sb", [P, NG0, T])
        w0_blocks = sb("w0_blocks", [P, NG0, NH])
        w0_diag = sb("w0_diag", [P, NG0, P])
        gh16 = sb("gh16", [P, 2, NT, P], F16)
        w1t = sb("w1t", [P, 2, KC, T], F16)
        w2t = sb("w2t", [P, 2, KC, T], F16)
        awt = sb("awt", [P, 2, KC, AW], F16)
        b2t = sb("b2t", [P, 2, T], F16)
        la16 = sb("la16", [P, 2, KC, NB, R], F16)
        lb16 = sb("lb16", [P, 2, NGA, T], F16)
        xt16 = sb("xt16", [P, 2, KC, NTOK], F16)
        lora_h = sb("lora_h", [P, NGA, TA])
        lora_h16 = sb("lora_h16", [P, 2, NGA, TA], F16)
        x2_sb = sb("x2_sb", [P, 2, NH, NB // 2])
        x2t16 = sb("x2t16", [P, 2, KC, NH, NB], F16)
        toep = sb("toep", [P, NH, 2, T], F16)
        zeros16 = sb("zeros16", [2 * NH, P], F16)

        arena = sb("arena", [P, KC * T + NB * KC * R + NGA * T])
        wide = [arena[:, 0:KC * T], arena[:, KC * T:KC * T + NB * KC * R], arena[:, KC * T + NB * KC * R:]]
        w1_nat = wide[0].rearrange("p (k i) -> p k i", k=KC)
        w2_nat = w1_nat
        out_sb = wide[0].rearrange("p (k i) -> p k i", i=T)
        la_sb = wide[1].rearrange("p (b j) -> p b j", b=NB)
        lb_sb = wide[2].rearrange("p (g o) -> p g o", g=NGA)

        toep_flat = toep[:, :, :, :].rearrange("p h c t -> p (h c t)").bitcast(F32)

        def table(i):
            return toep_flat[:, i * NTAB:(i + 1) * NTAB].rearrange("p (h l) -> p h l", h=NH)

        tab_th, tab_abs, tab_mag = table(0), table(1), table(2)
        tab_ki = table(3).bitcast(I32)

        K0 = 4 * NTAB
        trig_b = toep_flat[:, K0:K0 + NH * LB].rearrange("p (h b) -> p h b", h=NH)
        K0 += NH * LB
        cos_a = toep_flat[:, K0:K0 + NH * LA].rearrange("p (h a) -> p h a", h=NH)
        K0 += NH * LA
        sin_a = toep_flat[:, K0:K0 + NH * LA].rearrange("p (h a) -> p h a", h=NH)
        K0 += NH * LA
        k64 = toep_flat[0:LA, K0:K0 + NH * LB].rearrange("a (h b) -> a h b", h=NH)
        K0 += NH * LB
        k16 = toep_flat[0:LA, K0:K0 + NH * LB].bitcast(F16).rearrange("a (h c b) -> a h c b", h=NH, c=2)

        x2_flat = x2t16[:, :, :, :, :].rearrange("p c k h b -> p (c k h b)").bitcast(F32)
        x_flat = x_sb[:, :, :].rearrange("p g t -> p (g t)")
        a2_nat = x_flat[:, 0:T]
        wr_nat = x_flat[0:E, T:2 * T]
        b2_nat = x_flat[:, 2 * T:3 * T].rearrange("p (k e r) -> p k e r", k=KC, e=E)
        zcat = x2_flat[0:NH, 3 * T:3 * T + 8 * N].rearrange("h (i c n) -> h i c n", i=4, c=2)
        S0 = 3 * T + 8 * N
        SLOTS = 21
        small = x2_flat[0:NH, S0:S0 + SLOTS * (N + 1)].rearrange("h (i n) -> h i n", i=SLOTS)
        S0 += SLOTS * (N + 1)
        small_i = x2_flat[0:NH, S0:S0 + 3 * (N + 1)].bitcast(I32).rearrange("h (i n) -> h i n", i=3)
        S0 += 3 * (N + 1)
        b1_nat = x2_flat[0:KC, S0:S0 + P]

        sC = sb("sC", [NH, N, 2])
        sX = sb("sX", [NH, N + 1])
        sAi = sb("sAi", [NH, N])
        zt = sb("zt", [P, 4, NH])
        D_row = sb("D_row", [LA, NH])

        logit = sb("logit", [P, NT, E])
        top_v = sb("top_v", [P, NT, 8])
        top_i = sb("top_i", [P, NT, 8], U32)
        top_f = sb("top_f", [P, NT, 2])
        gdiff = sb("gdiff", [P, NT])
        gexp = sb("gexp", [P, NT])
        gsum = sb("gsum", [P, NT])
        grec = sb("grec", [P, NT])
        gw = sb("gw", [P, NT, 2])
        onehot = sb("onehot", [P, NT, 2, E])
        gates = sb("gates", [P, NT, E])
        gated_h = w0_diag
        conv_out = x2_sb[:, :, :, :].rearrange("p s h b -> p s (h b)")

        bank = [ctx.enter_context(nc.psum_tensor(f"bank{i}", [P, 512], F32)) for i in range(8)]

        full = [sem(f"psum_full{i}") for i in range(8)]
        free = [sem(f"psum_free{i}") for i in range(8)]
        unit = {}
        used = [0] * 8

        def add_unit(key, b):
            unit[key] = (b, used[b])
            used[b] += 1

        for k in range(KC):
            add_unit(("w1t", k), k)
        for g in range(NG0):
            add_unit(("l0", g), 4 + g % 4)
        add_unit(("z", 0), 0)
        for m in range(KC):
            add_unit(("l1", (m, 0)), m)
        for j in range(NGA):
            add_unit(("la", j), 4 + j)
        add_unit(("l1", (0, 1)), 4)
        add_unit(("k", 0), 0)
        add_unit(("k", 1), 1)
        add_unit(("l1", (1, 1)), 5)
        add_unit(("w2t", 0), 2)
        add_unit(("w2t", 1), 3)
        add_unit(("l1", (2, 1)), 6)
        add_unit(("w2t", 2), 0)
        add_unit(("w2t", 3), 1)
        add_unit(("a2t", 0), 2)
        add_unit(("wrt", 0), 3)
        add_unit(("b2t", 0), 0)
        add_unit(("l1", (3, 1)), 7)
        l1_order = [(m, n) for n in range(2) for m in range(KC)]
        for i in range(NT // 2):
            add_unit(("aw", i), (1, 2, 3, 0)[i])
        for t in range(NT):
            add_unit(("gt", t), 7)
            add_unit(("l2", t), 4 + t % 3)
        for t in range(NT):
            add_unit(("x3t", t), 2 + t % 2)
            add_unit(("conv", t), t % 2)

        def ps(key):
            return bank[unit[key][0]]

        def claim(eng, key):
            b, n = unit[key]
            if n:
                eng.wait_ge(free[b], n)

        def await_unit(eng, key):
            b, n = unit[key]
            eng.wait_ge(full[b], n + 1)

        def await_read(eng, key):
            b, n = unit[key]
            eng.wait_ge(free[b], n + 1)

        def full_of(key):
            return full[unit[key][0]]

        def free_of(key):
            return free[unit[key][0]]

        ids_in = sem("ids_in")
        cond_in = sem("cond_in")
        slot_in = sem("slot_in")
        x_in = [sem(f"x_in{g}") for g in range(NG0)]
        w1_in = sem("w1_in")
        w2_in = sem("w2_in")
        a2_in = sem("a2_in")
        b1_in = sem("b1_in")
        b2_in = sem("b2_in")
        bias_ready = sem("bias_ready")
        s4_in = sem("s4_in")
        la_in = sem("la_in")
        w0_in = [sem(f"w0_in{g}") for g in range(NG0)]
        lb_in = [sem(f"lb_in{j}") for j in range(NGA)]
        lane_ready = sem("lane_ready")
        steps_ready = sem("steps_ready")
        w0_index_ready = sem("w0_index_ready")
        lb_index_ready = sem("lb_index_ready")
        lora_zeroed = sem("lora_zeroed")
        ids_ready = sem("ids_ready")
        consts = sem("consts")
        pool_chain = sem("pool_chain")
        chain = sem("dve_chain")
        eye_added1 = sem("eye_added1")
        eye_added2 = sem("eye_added2")
        w0_ready = sem("w0_ready")
        w1t_hi = sem("w1t_hi")
        w1t_ready = sem("w1t_ready")
        half_angle = sem("half_angle")
        half_trig = sem("half_trig")
        z_ready = sem("z_ready")
        x1_hi = sem("x1_hi")
        x1_ready = sem("x1_ready")
        la_hi = sem("la_hi")
        la_ready = sem("la_ready")
        lb_hi = sem("lb_hi")
        lb_ready = sem("lb_ready")
        lh_hi = sem("lh_hi")
        lh_ready = sem("lh_ready")
        decay_ready = sem("decay_ready")
        mag_ready = sem("mag_ready")
        angle_ready = sem("angle_ready")
        trig_ready = sem("trig_ready")
        pq_ready = sem("pq_ready")
        k_scaled = sem("k_scaled")
        k_ready = sem("k_ready")
        k_put = sem("k_put")
        zeros_put = sem("zeros_put")
        toep_in = [sem(f"toep_in{g}") for g in range(NT)]
        w2_hi = sem("w2_hi")
        w2_ready = sem("w2_ready")
        x2_hi = sem("x2_hi")
        x2_ready = sem("x2_ready")
        gap_ready = sem("gap_ready")
        gexp_ready = sem("gexp_ready")
        gt_hi = sem("gt_hi")
        gt_ready = sem("gt_ready")
        x3t_hi = sem("x3t_hi")
        x3t_ready = sem("x3t_ready")
        out_ready = sem("out_ready")
        out_put = [sem(f"out_put{i}") for i in range(4)]

        block = ctx.enter_context(nc.Block())
        kern_rows = kern_dram.ap()

        @block.sync
        def _(sp):
            sp.dma_start(cond_bc[:, :], bass.AP(cond.tensor, 0, [[0, P], [1, NB]])).then_inc(cond_in, 16)
            sp.dma_start(slot_bc[:, :], bass.AP(slot.tensor, 0, [[0, P], [1, NB]])).then_inc(slot_in, 16)

            def load_x(g):
                sp.dma_start(x_sb[:, g, :], x[g * G0:(g + 1) * G0].rearrange("b c t -> (b c) t")).then_inc(x_in[g], 16)

            load_x(0)
            sp.dma_start(w1_nat[:, :, :], W1.rearrange("(k p) i -> p k i", p=P)).then_inc(w1_in, 16)
            for g in range(1, NG0):
                load_x(g)
            sp.wait_ge(slot_in, 16)
            for b0 in range(0, NB, GATHER):
                regs = [sp.alloc_register(f"slot{b0 + i}") for i in range(GATHER)]
                sp.load(regs, slot_bc[0:1, b0:b0 + GATHER])
                for i, reg in enumerate(regs):
                    row = sp.snap(reg, min_val=0, max_val=lora_A.shape[0] - 1)
                    sp.dma_start(la_sb[:, b0 + i, :],
                                 lora_A[bass.ds(row, 1)].rearrange("s (p k) r -> p (s k r)", p=P)).then_inc(la_in, 16)
            for k in range(KC):
                await_unit(sp, ("w1t", k))
            sp.dma_start(w2_nat[:, :, :], W2.rearrange("(k p) i -> p k i", p=P)).then_inc(w2_in, 16)
            for g in range(NG0):
                await_unit(sp, ("l0", g))
            sp.dma_start(a2_nat, A2.rearrange("e r i -> (e r) i")).then_inc(a2_in, 16)
            sp.dma_start(wr_nat, Wr).then_inc(a2_in, 16)
            for k in range(KC):
                sp.dma_start(b2_nat[:, k], B2[:, k * P:(k + 1) * P, :].rearrange("e p r -> p e r")).then_inc(b2_in, 16)
            sp.wait_ge(k_ready, 1)
            sp.dma_start(kern_rows[:, 0:T].rearrange("(h c) (a b) -> a (h c) b", c=2, b=LB),
                         k16[:, :, :, :].rearrange("a h c b -> a (h c) b")).then_inc(k_put, 16)
            sp.wait_ge(k_put, 16)
            sp.wait_ge(zeros_put, 16)
            for g in range(NT):
                rows = 2 * HT
                src = bass.AP(kern_rows.tensor, g * rows * KPAD, [[1, P], [KPAD, rows], [1, T]])
                sp.dma_start(toep[:, g * HT:(g + 1) * HT, :, :].rearrange("p h c t -> p (h c) t"),
                             src).then_inc(toep_in[g], 16)
            for t in range(NT):
                sp.wait_ge(out_ready, t + 1)
                for h in range(HT):
                    sp.dma_start(out[:, t * HT + h, :], out_sb[h * NB:(h + 1) * NB, t % 4, :]).then_inc(out_put[t % 4], 16)
            for i in range(4):
                sp.wait_ge(out_put[i], 16 * HT * (NT // 4))

        @block.gpsimd
        def _(pool):
            count = [0]

            def link(ins):
                count[0] += 1
                ins.then_inc(pool_chain, 1)
                pool.wait_ge(pool_chain, count[0])

            nc.gpsimd.iota(lane[:, :], pattern=[[0, 1]], base=0, channel_multiplier=1).then_inc(lane_ready, 1)
            for mask, blocks, rows, value in ((w0_mask, G0, NH, 1.0), (lora_mask, GA, R, 2.0 / WS)):
                link(nc.gpsimd.memset(mask[:, :, :], value))
                link(nc.gpsimd.affine_select(out=mask[:, :, :], in_=mask[:, :, :], compare_op=ALU.is_ge, fill=0.0, base=0,
                                             pattern=[[-rows, blocks], [0, NH]], channel_multiplier=1))
                nc.gpsimd.affine_select(out=mask[:, :, :], in_=mask[:, :, :], compare_op=ALU.is_ge, fill=0.0,
                                        base=rows - 1, pattern=[[rows, blocks], [0, NH]],
                                        channel_multiplier=-1).then_inc(consts, 1)
            link(nc.gpsimd.memset(ident[:, :], 0.0))
            nc.gpsimd.affine_select(out=ident[:, :], in_=ident[:, :], compare_op=ALU.not_equal, fill=1.0, base=0,
                                    pattern=[[-1, P]], channel_multiplier=1).then_inc(consts, 1)
            W0_rows = W0.rearrange("s c d -> (s c) d")
            pool.wait_ge(w0_index_ready, 1)
            for g in range(NG0):
                pool.indirect_dma_start(out=w0_blocks[:, g, :], out_offset=None, in_=W0_rows,
                                        in_offset=bass.IndirectOffsetOnAxis(w0_index[:, g:g + 1], 0)).then_inc(w0_in[g], 16)
            lb_rows = lora_B.rearrange("s r o -> (s r) o")
            pool.wait_ge(lb_index_ready, 1)
            for j in range(NGA):
                pool.indirect_dma_start(out=lb_sb[:, j, :], out_offset=None, in_=lb_rows,
                                        in_offset=bass.IndirectOffsetOnAxis(lb_index[:, j:j + 1], 0)).then_inc(lb_in[j], 16)
            nc.gpsimd.iota(powers_i[:, 0:LB], pattern=[[-1, LB]], base=LB - 1, channel_multiplier=0).then_inc(steps_ready, 1)
            nc.gpsimd.iota(powers_i[:, LB:NL], pattern=[[-LB, LA]], base=T - LB, channel_multiplier=0).then_inc(steps_ready, 1)
            nc.gpsimd.iota(steps_i, pattern=[[1, T]], base=0, channel_multiplier=0).then_inc(steps_ready, 1)
            nc.gpsimd.memset(lora_h[:, :, :], 0.0).then_inc(lora_zeroed, 1)
            link(nc.gpsimd.memset(zeros16[:, :], 0.0))
            pool.dma_start(kern_rows[:, T:], zeros16[:, :]).then_inc(zeros_put, 16)
            pool.wait_ge(steps_ready, 2)
            nc.gpsimd.tensor_copy(powers[:, :], powers_i[:, :]).then_inc(steps_ready, 1)
            pool.wait_ge(steps_ready, 4)
            await_read(pool, ("z", 0))
            nc.gpsimd.tensor_tensor(tab_th, zt[:, 1, :].unsqueeze(2).to_broadcast([P, NH, NL]),
                                    powers[:, :].unsqueeze(1).to_broadcast([P, NH, NL]), ALU.mult).then_inc(decay_ready, 1)
            nc.gpsimd.tensor_tensor(tab_mag, zt[:, 0, :].unsqueeze(2).to_broadcast([P, NH, NL]),
                                    powers[:, :].unsqueeze(1).to_broadcast([P, NH, NL]), ALU.mult).then_inc(decay_ready, 1)
            for j in range(NGA):
                pool.wait_ge(lh_hi, j + 1)
                nc.gpsimd.tensor_tensor(lora_h16[:, 1, j, :], lora_h[:, j, :], lora_h16[:, 0, j, :],
                                        ALU.subtract).then_inc(lh_ready, 1)
            for i, (m, n) in enumerate(l1_order):
                pool.wait_ge(x2_hi, i + 1)
                dst = x2t16[:, :, m, :, n * (NB // 2):(n + 1) * (NB // 2)]
                nc.gpsimd.tensor_tensor(dst[:, 1], x2_sb[:, i % 2], dst[:, 0], ALU.subtract).then_inc(x2_ready, 1)
            for t in range(NT):
                await_read(pool, ("conv", t))
                if t >= 4:
                    pool.wait_ge(out_put[t % 4], 16 * HT * (t // 4))
                nc.gpsimd.tensor_tensor(out_sb[:, t % 4, :], conv_out[:, t % 2, :], x_sb[:, t, :],
                                        ALU.add).then_inc(out_ready, 1)

        @block.scalar
        def _(act):
            act.dma_start(sX[:, 0:N], log_A_real).then_inc(s4_in, 16)
            act.dma_start(sX[:, N:N + 1], log_dt.rearrange("(h a) -> h a", a=1)).then_inc(s4_in, 16)
            act.dma_start(sAi[:, :], A_imag).then_inc(s4_in, 16)
            act.dma_start(sC[:, :, :], C).then_inc(s4_in, 16)
            act.dma_start(D_row[:, :], bass.AP(D.tensor, 0, [[0, LA], [1, NH]])).then_inc(s4_in, 16)
            act.dma_start(ids_i[:, 0:1], lang.rearrange("(b a) -> b a", a=1)).then_inc(ids_in, 16)
            act.dma_start(ids_i[:, 1:2], length.rearrange("(b a) -> b a", a=1)).then_inc(ids_in, 16)
            act.dma_start(b1_nat, b1.rearrange("(k p) -> k p", p=P)).then_inc(b1_in, 16)

            for k in range(KC):
                await_unit(act, ("w1t", k))
                nc.scalar.activation(w1t[:, 0, k, :], ps(("w1t", k))[:, :], ACT.Copy, scale=WS).then_inc(w1t_hi, 1)
            act.wait_ge(half_angle, 2)
            nc.scalar.activation(small[:, 10, 0:N], small[:, 8, 0:N], ACT.Sin).then_inc(half_trig, 1)
            nc.scalar.activation(small[:, 11, 0:N], small[:, 9, 0:N], ACT.Sin).then_inc(half_trig, 1)
            for g in range(NG0):
                await_unit(act, ("l0", g))
                nc.scalar.activation(xt16[:, 0, :, g * P:(g + 1) * P],
                                     ps(("l0", g))[:, :].rearrange("p (k n) -> p k n", k=KC), ACT.Copy).then_inc(x1_hi, 1)
            act.wait_ge(la_in, 16 * NB)
            for j in range(NGA):
                B = slice(j * GA, (j + 1) * GA)
                nc.scalar.activation(la16[:, 0, :, B], la_sb[:, B, :].rearrange("p b (k r) -> p k b r", k=KC),
                                     ACT.Copy, scale=WS).then_inc(la_hi, 1)
            for j in range(NGA):
                act.wait_ge(lb_in[j], 16)
                nc.scalar.activation(lb16[:, 0, j, :], lb_sb[:, j, :], ACT.Copy, scale=WS).then_inc(lb_hi, 1)
            act.wait_ge(decay_ready, 2)
            nc.scalar.activation(tab_mag, tab_mag, ACT.Exp).then_inc(mag_ready, 1)
            act.wait_ge(angle_ready, 2)
            nc.scalar.activation(trig_b[0:N], tab_abs[0:N, :, 0:LB], ACT.Sin, bias=half_pi[0:N, :],
                                 scale=-1.0).then_inc(trig_ready, 1)
            nc.scalar.activation(trig_b[N:P], tab_th[N:P, :, 0:LB], ACT.Sin).then_inc(trig_ready, 1)
            nc.scalar.activation(cos_a, tab_abs[:, :, LB:NL], ACT.Sin, bias=half_pi[:, :],
                                 scale=-1.0).then_inc(trig_ready, 1)
            nc.scalar.activation(sin_a, tab_th[:, :, LB:NL], ACT.Sin).then_inc(trig_ready, 1)
            for j in range(NGA):
                await_read(act, ("la", j))
                nc.scalar.activation(lora_h16[:, 0, j, :], lora_h[:, j, :], ACT.Copy).then_inc(lh_hi, 1)

            def w2t_high(k):
                await_unit(act, ("w2t", k))
                nc.scalar.activation(w2t[:, 0, k, :], ps(("w2t", k))[:, :], ACT.Copy, scale=WS).then_inc(w2_hi, 1)

            def small2_high():
                await_unit(act, ("a2t", 0))
                nc.scalar.activation(awt[:, 0, :, 0:P], ps(("a2t", 0))[:, :].rearrange("p (k n) -> p k n", k=KC),
                                     ACT.Copy, scale=WS).then_inc(w2_hi, 1)
                await_unit(act, ("wrt", 0))
                nc.scalar.activation(awt[:, 0, :, P:AW], ps(("wrt", 0))[:, 0:KC * E].rearrange("p (k n) -> p k n", k=KC),
                                     ACT.Copy, scale=WS).then_inc(w2_hi, 1)
                await_unit(act, ("b2t", 0))
                nc.scalar.activation(b2t[:, 0, :], ps(("b2t", 0))[:, :], ACT.Copy, scale=WS).then_inc(w2_hi, 1)

            act.wait_ge(bias_ready, 1)
            for i, (m, n) in enumerate(l1_order):
                await_unit(act, ("l1", (m, n)))
                if i >= 2:
                    act.wait_ge(x2_ready, i - 1)
                nc.scalar.activation(x2_sb[:, i % 2], ps(("l1", (m, n)))[:, :].rearrange("p (b h) -> p h b", h=NH),
                                     ACT.Identity, bias=bias_sb[:, m:m + 1],
                                     scale=1.0 / WS).then_inc(free_of(("l1", (m, n))), 1)
                await_read(act, ("l1", (m, n)))
                nc.scalar.activation(x2t16[:, 0, m, :, n * (NB // 2):(n + 1) * (NB // 2)], x2_sb[:, i % 2],
                                     ACT.Copy).then_inc(x2_hi, 1)
                if (m, n) == (1, 1):
                    w2t_high(0)
                    w2t_high(1)
                if (m, n) == (2, 1):
                    w2t_high(2)
                    w2t_high(3)
                    small2_high()
            for s in range(2):
                act.wait_ge(gap_ready, s + 1)
                nc.scalar.activation(gexp[:, s * 4:s * 4 + 4], gdiff[:, s * 4:s * 4 + 4], ACT.Exp).then_inc(gexp_ready, 1)


            def gh_high(t):
                await_unit(act, ("gt", t))
                nc.scalar.activation(gh16[:, 0, t, :], ps(("gt", t))[:, 0:P], ACT.Copy).then_inc(gt_hi, 1)

            def x3_sum(t):
                await_unit(act, ("l2", t))
                nc.scalar.activation(x_sb[:, t, :], ps(("l2", t))[:, :], ACT.Copy, scale=1.0 / WS).then_inc(free_of(("l2", t)), 1)

            def x3t_high(t):
                await_unit(act, ("x3t", t))
                nc.scalar.activation(xt16[:, 0, :, t * P:(t + 1) * P],
                                     ps(("x3t", t))[:, :].rearrange("p (k n) -> p k n", k=KC), ACT.Copy).then_inc(x3t_hi, 1)

            for i in range(NT + 2):
                if i < NT:
                    gh_high(i)
                if 1 <= i <= NT:
                    x3_sum(i - 1)
                if i >= 2:
                    x3t_high(i - 2)

        @block.vector
        def _(dve):
            count = [0]
            V = nc.vector

            def link(ins):
                count[0] += 1
                ins.then_inc(chain, 1)
                dve.wait_ge(chain, count[0])

            def exp_parts(src, w, slot0, islot):
                ki, p2 = small_i[:, islot, 0:w], small_i[:, islot + 1, 0:w]
                r, q = small[:, slot0, 0:w], small[:, slot0 + 1, 0:w]
                link(V.tensor_scalar(ki, src, 1.0 / math.log(2.0), None, ALU.mult))
                link(V.scalar_tensor_tensor(r, ki, -LN2_HI, src, ALU.mult, ALU.add))
                link(V.scalar_tensor_tensor(r, ki, -LN2_LO, r, ALU.mult, ALU.add))
                link(V.tensor_scalar(q, r, 1.0 / math.factorial(EXP_TERMS), None, ALU.mult))
                for n in range(EXP_TERMS - 1, 0, -1):
                    link(V.scalar_tensor_tensor(q, q, 1.0 / math.factorial(n), r, ALU.add, ALU.mult))
                link(V.tensor_scalar(p2, ki, 127.0, 0.0, ALU.add, ALU.max))
                link(V.tensor_scalar(p2, p2, 23, None, ALU.logical_shift_left))
                return q, p2.bitcast(F32)

            def reduce_angle(th, ki):
                link(V.tensor_scalar(ki, th, 1.0 / TWO_PI, None, ALU.mult))
                for part in (PI_HI, PI_LO):
                    link(V.scalar_tensor_tensor(th, ki, -part, th, ALU.mult, ALU.add))
                link(V.tensor_scalar(th, th, PI_DOWN, -PI_DOWN, ALU.min, ALU.max))

            V.memset(half_pi[:, :], math.pi / 2)
            dve.wait_ge(cond_in, 16)
            dve.wait_ge(consts, 1)
            link(V.tensor_tensor(cond_own[:, :, :], cond_bc[:, :].rearrange("p (g b) -> p g b", g=NG0),
                                 w0_mask[:, :, 0].unsqueeze(1).to_broadcast([P, NG0, G0]), ALU.mult))
            link(V.reduce_sum(cond_sum[:, :], cond_own[:, :, :], axis=mybir.AxisListType.X))
            dve.wait_ge(lane_ready, 1)
            link(V.tensor_scalar(lane_mod[:, 0:1], lane[:, :], NH - 1, None, ALU.bitwise_and))
            link(V.tensor_scalar(lane_mod[:, 1:2], lane[:, :], R - 1, None, ALU.bitwise_and))
            V.scalar_tensor_tensor(w0_index[:, :], cond_sum[:, :], float(NH), lane_mod[:, 0:1].to_broadcast([P, NG0]),
                                   ALU.mult, ALU.add).then_inc(w0_index_ready, 1)
            dve.wait_ge(slot_in, 16)
            dve.wait_ge(consts, 2)
            link(V.tensor_tensor(slot_own[:, :, :], slot_bc[:, :].rearrange("p (g b) -> p g b", g=NGA),
                                 lora_mask[:, :, 0].unsqueeze(1).to_broadcast([P, NGA, GA]), ALU.mult))
            link(V.reduce_sum(slot_sum[:, :], slot_own[:, :, :], axis=mybir.AxisListType.X))
            V.scalar_tensor_tensor(lb_index[:, :], slot_sum[:, :], R * WS / 2.0, lane_mod[:, 1:2].to_broadcast([P, NGA]),
                                   ALU.mult, ALU.add).then_inc(lb_index_ready, 1)
            dve.wait_ge(s4_in, 16 * 5)
            q, p2 = exp_parts(sX[:, :], N + 1, 0, 0)
            rates = small[:, 2, :]
            link(V.scalar_tensor_tensor(rates, q, 1.0, p2, ALU.add, ALU.mult))
            rate, dt = small[:, 2, 0:N], small[:, 2, N:N + 1]
            dre, dim = small[:, 3, 0:N], small[:, 4, 0:N]
            link(V.tensor_scalar(dre, rate, dt, -1.0, ALU.mult, ALU.mult))
            link(V.tensor_scalar(dim, sAi[:, :], dt, None, ALU.mult))
            ha, hc = small[:, 8, 0:N], small[:, 9, 0:N]
            link(V.tensor_scalar(ha, dim, 0.5, None, ALU.mult))
            reduce_angle(ha, small_i[:, 2, 0:N])
            link(V.tensor_scalar(hc, ha, -1.0, None, ALU.mult))
            link(V.tensor_tensor(hc, hc, ha, ALU.min))
            V.tensor_scalar(hc, hc, math.pi / 2, None, ALU.add).then_inc(half_angle, 2)
            dve.wait_ge(w1_in, 16)
            dve.wait_ge(consts, 3)
            for k in range(KC):
                d = w1_nat[:, k, k * P:(k + 1) * P]
                V.tensor_tensor(d, d, ident[:, :], ALU.add).then_inc(eye_added1, 1)
            for g in range(NG0):
                dve.wait_ge(w0_in[g], 16)
                link(V.tensor_tensor(w0_diag[:, g, :].rearrange("p (b d) -> p b d", b=G0),
                                     w0_blocks[:, g, :].unsqueeze(1).to_broadcast([P, G0, NH]), w0_mask[:, :, :], ALU.mult))
                V.tensor_tensor(w0_diag[:, g, :], w0_diag[:, g, :], ident[:, :], ALU.add).then_inc(w0_ready, 1)
            q, p2 = exp_parts(dre, N, 5, 0)
            em1, e1 = small[:, 7, 0:N], small[:, 12, 0:N]
            link(V.tensor_scalar(e1, p2, -1.0, None, ALU.add))
            link(V.tensor_tensor(em1, q, p2, ALU.mult))
            link(V.tensor_tensor(em1, em1, e1, ALU.add))
            link(V.tensor_scalar(e1, em1, 1.0, None, ALU.add))
            dve.wait_ge(half_trig, 2)
            sn, cs = small[:, 10, 0:N], small[:, 11, 0:N]
            t0, t1, t2, er, ei = (small[:, i, 0:N] for i in (13, 14, 15, 16, 17))
            fr, fi, inv = (small[:, i, 0:N] for i in (18, 19, 20))
            link(V.tensor_tensor(t0, sn, sn, ALU.mult))
            link(V.tensor_tensor(t0, t0, e1, ALU.mult))
            link(V.scalar_tensor_tensor(er, t0, -2.0, em1, ALU.mult, ALU.add))
            link(V.tensor_tensor(t1, sn, cs, ALU.mult))
            link(V.scalar_tensor_tensor(ei, t1, 2.0, e1, ALU.mult, ALU.mult))
            link(V.tensor_tensor(t0, rate, rate, ALU.mult))
            link(V.tensor_tensor(t1, sAi[:, :], sAi[:, :], ALU.mult))
            link(V.tensor_tensor(t0, t0, t1, ALU.add))
            link(V.reciprocal(inv, t0))
            link(V.scalar_tensor_tensor(t0, er, -1.0, rate, ALU.mult, ALU.mult))
            link(V.tensor_tensor(t1, ei, sAi[:, :], ALU.mult))
            link(V.tensor_tensor(fr, t0, t1, ALU.add))
            link(V.scalar_tensor_tensor(t0, ei, -1.0, rate, ALU.mult, ALU.mult))
            link(V.tensor_tensor(t1, er, sAi[:, :], ALU.mult))
            link(V.tensor_tensor(fi, t0, t1, ALU.subtract))
            link(V.scalar_tensor_tensor(fr, fr, 2.0, inv, ALU.mult, ALU.mult))
            link(V.scalar_tensor_tensor(fi, fi, 2.0, inv, ALU.mult, ALU.mult))
            cr, ci = sC[:, :, 0], sC[:, :, 1]
            link(V.tensor_tensor(t0, cr, fr, ALU.mult))
            link(V.tensor_tensor(t1, ci, fi, ALU.mult))
            link(V.tensor_tensor(zcat[:, 2, 0, :], t0, t1, ALU.subtract))
            link(V.tensor_tensor(t2, cr, fi, ALU.mult))
            link(V.tensor_tensor(t0, ci, fr, ALU.mult))
            link(V.scalar_tensor_tensor(zcat[:, 2, 1, :], t2, -1.0, t0, ALU.mult, ALU.subtract))
            link(V.tensor_copy(zcat[:, 3, 0, :], zcat[:, 2, 1, :]))
            link(V.tensor_scalar(zcat[:, 3, 1, :], zcat[:, 2, 0, :], -1.0, None, ALU.mult))
            for half in range(2):
                V.tensor_copy(zcat[:, 0, half, :], dre).then_inc(z_ready, 1)
                V.tensor_copy(zcat[:, 1, half, :], dim).then_inc(z_ready, 1)
            for k in range(KC):
                dve.wait_ge(w1t_hi, k + 1)
                V.scalar_tensor_tensor(w1t[:, 1, k, :], ps(("w1t", k))[:, :], WS, w1t[:, 0, k, :],
                                       ALU.mult, ALU.subtract).then_inc(free_of(("w1t", k)), 1)
            for g in range(NG0):
                dve.wait_ge(x1_hi, g + 1)
                V.tensor_tensor(xt16[:, 1, :, g * P:(g + 1) * P], ps(("l0", g))[:, :].rearrange("p (k n) -> p k n", k=KC),
                                xt16[:, 0, :, g * P:(g + 1) * P], ALU.subtract).then_inc(free_of(("l0", g)), 1)
            await_unit(dve, ("z", 0))
            V.tensor_copy(bias_sb[:, :], ps(("z", 0))[:, 4 * NH:4 * NH + KC]).then_inc(bias_ready, 1)
            V.tensor_copy(zt[:, :, :].rearrange("p a h -> p (a h)"), ps(("z", 0))[:, 0:4 * NH]).then_inc(free_of(("z", 0)), 1)
            for j in range(NGA):
                dve.wait_ge(la_hi, j + 1)
                B = slice(j * GA, (j + 1) * GA)
                for k in range(KC):
                    ins = V.scalar_tensor_tensor(la16[:, 1, k, B], la_sb[:, B, k * R:(k + 1) * R], WS, la16[:, 0, k, B],
                                                 ALU.mult, ALU.subtract)
                ins.then_inc(la_ready, 1)
            for j in range(NGA):
                dve.wait_ge(lb_hi, j + 1)
                V.scalar_tensor_tensor(lb16[:, 1, j, :], lb_sb[:, j, :], WS, lb16[:, 0, j, :],
                                       ALU.mult, ALU.subtract).then_inc(lb_ready, 1)
            dve.wait_ge(decay_ready, 1)
            reduce_angle(tab_th, tab_ki)
            V.scalar_tensor_tensor(tab_abs, tab_th, -1.0, tab_th, ALU.mult, ALU.max).then_inc(angle_ready, 2)
            dve.wait_ge(w2_in, 16)
            for k in range(KC):
                d = w2_nat[:, k, k * P:(k + 1) * P]
                V.tensor_tensor(d, d, ident[:, :], ALU.add).then_inc(eye_added2, 1)
            dve.wait_ge(lora_zeroed, 1)
            for j in range(NGA):
                await_unit(dve, ("la", j))
                for q in range(2):
                    rows, bs = slice(q * N, (q + 1) * N), slice(q * G0, (q + 1) * G0)
                    ins = V.tensor_tensor(lora_h[rows, j, q * P:(q + 1) * P], ps(("la", j))[rows, 0:P],
                                          lora_mask[rows, bs, :].rearrange("p b h -> p (b h)"), ALU.mult)
                ins.then_inc(free_of(("la", j)), 1)
            dve.wait_ge(mag_ready, 1)
            dve.wait_ge(trig_ready, 4)
            V.tensor_tensor(trig_b, trig_b, tab_mag[:, :, 0:LB], ALU.mult).then_inc(pq_ready, 1)
            link(V.tensor_tensor(cos_a, cos_a,
                                 zt[:, 2, :].unsqueeze(2).to_broadcast([P, NH, LA]), ALU.mult))
            link(V.tensor_tensor(sin_a, sin_a,
                                 zt[:, 3, :].unsqueeze(2).to_broadcast([P, NH, LA]), ALU.mult))
            link(V.tensor_tensor(cos_a, cos_a, sin_a, ALU.add))
            V.tensor_tensor(cos_a, cos_a, tab_mag[:, :, LB:NL], ALU.mult).then_inc(pq_ready, 1)
            HH = NH // 2
            for s in range(2):
                await_unit(dve, ("k", s))
                V.tensor_scalar(k64[:, s * HH:(s + 1) * HH, :].rearrange("a h b -> a (h b)"), ps(("k", s))[0:LA, :], WS,
                                None, ALU.mult).then_inc(free_of(("k", s)), 1)
            await_read(dve, ("k", 0))
            await_read(dve, ("k", 1))
            link(V.tensor_scalar(D_row[:, :], D_row[:, :], ident[0:LA, LA - 1:LA], WS, ALU.mult, ALU.mult))
            link(V.tensor_tensor(k64[:, :, LB - 1], k64[:, :, LB - 1], D_row[:, :], ALU.add))
            link(V.tensor_copy(k16[:, :, 0, :], k64[:, :, :]))
            V.tensor_tensor(k16[:, :, 1, :], k64[:, :, :], k16[:, :, 0, :], ALU.subtract).then_inc(k_ready, 1)

            dve.wait_ge(ids_in, 16 * 2)
            dve.wait_ge(steps_ready, 4)
            for q in range(HT):
                V.tensor_copy(ids[q * NB:(q + 1) * NB, :], ids_i[:, :]).then_inc(ids_ready, 1)
            link(V.tensor_copy(steps[:, :], steps_i))
            dve.wait_ge(ids_ready, HT)
            V.tensor_scalar(conv_mask[:, :], steps[:, :], ids[:, 1:2], 1.0 / WS, ALU.is_lt, ALU.mult)
            V.tensor_scalar(lang_bias[:, :], steps[:, 0:E], ids[:, 0:1], 5.0, ALU.is_equal, ALU.mult)
            for k in range(KC):
                dve.wait_ge(w2_hi, k + 1)
                V.scalar_tensor_tensor(w2t[:, 1, k, :], ps(("w2t", k))[:, :], WS, w2t[:, 0, k, :],
                                       ALU.mult, ALU.subtract).then_inc(free_of(("w2t", k)), 1)
            dve.wait_ge(w2_hi, KC + 1)
            V.scalar_tensor_tensor(awt[:, 1, :, 0:P], ps(("a2t", 0))[:, :].rearrange("p (k n) -> p k n", k=KC), WS,
                                   awt[:, 0, :, 0:P], ALU.mult, ALU.subtract).then_inc(free_of(("a2t", 0)), 1)
            dve.wait_ge(w2_hi, KC + 2)
            V.scalar_tensor_tensor(awt[:, 1, :, P:AW], ps(("wrt", 0))[:, 0:KC * E].rearrange("p (k n) -> p k n", k=KC), WS,
                                   awt[:, 0, :, P:AW], ALU.mult, ALU.subtract).then_inc(free_of(("wrt", 0)), 1)
            dve.wait_ge(w2_hi, KC + 3)
            V.scalar_tensor_tensor(b2t[:, 1, :], ps(("b2t", 0))[:, :], WS, b2t[:, 0, :],
                                   ALU.mult, ALU.subtract).then_inc(free_of(("b2t", 0)), 1)

            def logits(t):
                await_unit(dve, ("aw", t // 2))
                at = (t % 2) * AW
                link(V.scalar_tensor_tensor(logit[:, t, :], ps(("aw", t // 2))[:, at + P:at + AW], 1.0 / WS,
                                            lang_bias[:, :], ALU.mult, ALU.add))
                link(V.max(top_v[:, t, :], logit[:, t, :]))
                link(V.max_index(top_i[:, t, :], top_v[:, t, :], logit[:, t, :]))

            for s in range(2):
                S = slice(s * 4, s * 4 + 4)
                for t in range(s * 4, s * 4 + 4):
                    logits(t)
                V.tensor_tensor(gdiff[:, S], top_v[:, S, 1], top_v[:, S, 0], ALU.subtract).then_inc(gap_ready, 1)
                link(V.tensor_copy(top_f[:, S, :], top_i[:, S, 0:2]))
                link(V.tensor_tensor(onehot[:, S], steps[:, 0:E].unsqueeze(1).unsqueeze(1).to_broadcast([P, 4, 2, E]),
                                     top_f[:, S, :].unsqueeze(3).to_broadcast([P, 4, 2, E]), ALU.is_equal))
                dve.wait_ge(gexp_ready, s + 1)
                link(V.tensor_scalar(gsum[:, S], gexp[:, S], 1.0, None, ALU.add))
                link(V.reciprocal(grec[:, S], gsum[:, S]))
                link(V.tensor_scalar(gw[:, S, 0], grec[:, S], 2.0 / WS, None, ALU.mult))
                link(V.tensor_tensor(gw[:, S, 1], gw[:, S, 0], gexp[:, S], ALU.mult))
                link(V.tensor_tensor(onehot[:, S], onehot[:, S], gw[:, S, :].unsqueeze(3).to_broadcast([P, 4, 2, E]), ALU.mult))
                link(V.tensor_tensor(gates[:, S, :], onehot[:, S, 0, :], onehot[:, S, 1, :], ALU.add))
                for t in range(s * 4, s * 4 + 4):
                    at = (t % 2) * AW
                    ins = V.tensor_tensor(gated_h[:, t, :].rearrange("p (e r) -> p e r", e=E),
                                          ps(("aw", t // 2))[:, at:at + P].rearrange("p (e r) -> p e r", e=E),
                                          gates[:, t, :].unsqueeze(2).to_broadcast([P, E, R]), ALU.mult)
                    if t % 2 == 1:
                        ins.then_inc(free_of(("aw", t // 2)), 1)

            def gh_low(t):
                dve.wait_ge(gt_hi, t + 1)
                V.tensor_tensor(gh16[:, 1, t, :], ps(("gt", t))[:, 0:P], gh16[:, 0, t, :],
                                ALU.subtract).then_inc(free_of(("gt", t)), 1)

            def x3t_low(t):
                dve.wait_ge(x3t_hi, t + 1)
                V.tensor_tensor(xt16[:, 1, :, t * P:(t + 1) * P], ps(("x3t", t))[:, :].rearrange("p (k n) -> p k n", k=KC),
                                xt16[:, 0, :, t * P:(t + 1) * P], ALU.subtract).then_inc(free_of(("x3t", t)), 1)

            def mask_conv(t):
                await_unit(dve, ("conv", t))
                if t >= 2:
                    dve.wait_ge(out_ready, t - 1)
                V.tensor_tensor(conv_out[:, t % 2, :], ps(("conv", t))[:, T - 1::-1], conv_mask[:, :],
                                ALU.mult).then_inc(free_of(("conv", t)), 1)

            for i in range(NT + 4):
                if i < NT:
                    gh_low(i)
                if 2 <= i < NT + 2:
                    x3t_low(i - 2)
                if i >= 4:
                    mask_conv(i - 4)

        @block.tensor
        def _(pe):
            mm = nc.tensor.matmul

            def transposes(key, sources, width, rows=P):
                claim(pe, key)
                for i, src in enumerate(sources):
                    last = nc.tensor.transpose(ps(key)[:, i * width:(i + 1) * width], src, ident[0:rows, 0:rows])
                last.then_inc(full_of(key), 1)

            pe.wait_ge(eye_added1, KC)
            for k in range(KC):
                transposes(("w1t", k), [w1_nat[:, m, k:T:KC] for m in range(KC)], P)
            for g in range(NG0):
                pe.wait_ge(w0_ready, g + 1)
                pe.wait_ge(x_in[g], 16)
                claim(pe, ("l0", g))
                for k in range(KC):
                    last = mm(ps(("l0", g))[:, k * P:(k + 1) * P], x_sb[:, g, k:T:KC], w0_diag[:, g, :],
                              start=True, stop=True)
                last.then_inc(full_of(("l0", g)), 1)
            pe.wait_ge(z_ready, 4)
            pe.wait_ge(b1_in, 16)
            claim(pe, ("z", 0))
            nc.tensor.transpose(ps(("z", 0))[:, 4 * NH:4 * NH + KC], b1_nat, ident[0:KC, 0:KC])
            transposes(("z", 0), [zcat[:, i].rearrange("h c n -> h (c n)") for i in range(4)], NH, NH)

            def product(dst, pairs, first=True, final=True):
                n = len(pairs) * len(PARTS_USED)
                i = 0
                for lhs, rhs in pairs:
                    for a, b in PARTS_USED:
                        last = mm(dst, lhs(a), rhs(b), start=first and i == 0, stop=final and i == n - 1)
                        i += 1
                return last

            def l1_main(m, n):
                key = ("l1", (m, n))
                claim(pe, key)
                M = slice(m * P, (m + 1) * P)
                pairs = [(lambda a, k=k: w1t[:, a, k, M], lambda b, k=k: xt16[:, b, k, n * HALF:(n + 1) * HALF])
                         for k in range(KC)]
                product(ps(key)[:, :], pairs, final=False)

            def l1_lora(m, n):
                key = ("l1", (m, n))
                M = slice(m * P, (m + 1) * P)
                per = HALF // TA
                for j in range(n * per, (n + 1) * per):
                    pe.wait_ge(lb_ready, j + 1)
                    pe.wait_ge(lh_ready, j + 1)
                    c = (j - n * per) * TA
                    pairs = [(lambda a: lb16[:, a, j, M], lambda b: lora_h16[:, b, j, :])]
                    last = product(ps(key)[:, c:c + TA], pairs, first=False, final=(j == (n + 1) * per - 1))
                last.then_inc(full_of(key), 1)

            for k in range(KC):
                await_read(pe, ("w1t", k))
            for g in range(NG0 // 2):
                await_read(pe, ("l0", g))
            for m in range(KC):
                l1_main(m, 0)
            for j in range(NGA):
                key = ("la", j)
                pe.wait_ge(la_ready, j + 1)
                claim(pe, key)
                for g in range(2 * j, 2 * j + 2):
                    await_read(pe, ("l0", g))
                for k in range(KC):
                    for n, (a, b) in enumerate(PARTS_USED):
                        for q in range(2):
                            b0 = j * GA + q * G0
                            last = mm(ps(key)[q * N:(q + 1) * N, 0:P],
                                      la16[:, a, k, b0:b0 + G0, :].rearrange("p b r -> p (b r)"),
                                      xt16[:, b, k, b0 * NH:b0 * NH + P], start=(k == 0 and n == 0),
                                      stop=(k == KC - 1 and n == 2))
                last.then_inc(full_of(key), 1)
            for m in range(KC):
                l1_lora(m, 0)
            l1_main(0, 1)
            l1_lora(0, 1)
            pe.wait_ge(pq_ready, 2)
            for s in range(2):
                claim(pe, ("k", s))
                for h in range(NH // 2):
                    hh = s * (NH // 2) + h
                    last = mm(ps(("k", s))[0:LA, h * LB:(h + 1) * LB], cos_a[:, hh, :], trig_b[:, hh, :],
                              start=True, stop=True)
                last.then_inc(full_of(("k", s)), 1)
            l1_main(1, 1)
            l1_lora(1, 1)
            pe.wait_ge(eye_added2, KC)
            for k in range(2):
                transposes(("w2t", k), [w2_nat[:, m, k * P:(k + 1) * P] for m in range(KC)], P)
            l1_main(2, 1)
            l1_lora(2, 1)
            for k in range(2, KC):
                transposes(("w2t", k), [w2_nat[:, m, k * P:(k + 1) * P] for m in range(KC)], P)
            pe.wait_ge(a2_in, 32)
            transposes(("a2t", 0), [a2_nat[:, k * P:(k + 1) * P] for k in range(KC)], P)
            transposes(("wrt", 0), [wr_nat[:, k * P:(k + 1) * P] for k in range(KC)], E, E)
            pe.wait_ge(b2_in, 16 * KC)
            transposes(("b2t", 0), [b2_nat[:, k].rearrange("p e r -> p (e r)") for k in range(KC)], P)
            l1_main(3, 1)
            l1_lora(3, 1)
            def x2_part(a, k, t):
                return x2t16[:, a, k, t * HT:(t + 1) * HT, :].rearrange("p h b -> p (h b)")

            def down(t):
                key = ("aw", t // 2)
                if t % 2 == 0:
                    claim(pe, key)
                at = (t % 2) * AW
                for k in range(KC):
                    if t == 0:
                        pe.wait_ge(x2_ready, KC + k + 1)
                    last = product(ps(key)[:, at:at + AW],
                                   [(lambda a: x2_part(a, k, t), lambda b: awt[:, b, k, :])],
                                   first=(k == 0), final=(k == KC - 1))
                if t % 2 == 1:
                    last.then_inc(full_of(key), 1)

            def main2(t):
                key = ("l2", t)
                claim(pe, key)
                product(ps(key)[:, :], [(lambda a, k=k: x2_part(a, k, t), lambda b, k=k: w2t[:, b, k, :])
                                        for k in range(KC)], final=False)

            def turn_gated(t):
                claim(pe, ("gt", t))
                await_read(pe, ("aw", t // 2))
                nc.tensor.transpose(ps(("gt", t))[:, 0:P], gated_h[:, t, :], ident[:, :]).then_inc(full_of(("gt", t)), 1)

            def up(t):
                await_read(pe, ("gt", t))
                product(ps(("l2", t))[:, :], [(lambda a: gh16[:, a, t, :], lambda b: b2t[:, b, :])],
                        first=False).then_inc(full_of(("l2", t)), 1)

            def turn3(t):
                await_read(pe, ("l2", t))
                transposes(("x3t", t), [x_sb[:, t, k * P:(k + 1) * P] for k in range(KC)], P)

            def conv(t):
                key = ("conv", t)
                claim(pe, key)
                await_read(pe, ("x3t", t))
                pe.wait_ge(toep_in[t], 16)
                for k in range(KC):
                    for n, (a, b) in enumerate(PARTS_USED):
                        for h in range(HT):
                            rows = slice(h * NB, (h + 1) * NB)
                            last = mm(ps(key)[rows, 0:T - k * P], xt16[:, a, k, t * P + h * NB:t * P + (h + 1) * NB],
                                      toep[:, t * HT + h, b, k * P:T], start=(k == 0 and n == 0),
                                      stop=(k == KC - 1 and n == 2))
                last.then_inc(full_of(key), 1)

            for key in [("a2t", 0), ("wrt", 0)]:
                await_read(pe, key)
            for t in range(NT // 2):
                down(t)
            for key in [("w2t", k) for k in range(KC)] + [("b2t", 0)]:
                await_read(pe, key)
            main2(0)
            for t in range(NT // 2, NT):
                down(t)
            for i in range(1, NT + 3):
                if i <= NT:
                    turn_gated(i - 1)
                if i < NT:
                    main2(i)
                if i <= NT:
                    up(i - 1)
                if 2 <= i <= NT + 1:
                    turn3(i - 2)
                if i >= 3:
                    conv(i - 3)


_INS = ['x', 'itok_B_0_15', 'itok_B_0_23', 'itok_B_0_7', 'itok_B_8_3872', 'L0_cond_weights', 'L1_cond_W', 'L1_cond_b',
        'L1_cond_lora_As', 'L1_cond_lora_Bs', 'L2_cond_W', 'L2_cond_Wr', 'L2_cond_A', 'L2_cond_B', 'L3_cond_log_dt',
        'L3_cond_C', 'L3_cond_log_A_real', 'L3_cond_A_imag', 'L3_cond_D']


def kernel(**inputs):
    import numpy as _np
    import concourse.bacc as _bacc
    from concourse import mybir as _mybir
    from concourse.bass_utils import run_bass_kernel_spmd as _run

    nc = _bacc.Bacc("TRN2", target_bir_lowering=False, num_devices=1)
    arrays, args = {}, []
    for name in _INS:
        a = _np.ascontiguousarray(inputs[name])
        arrays[f"in_{name}_dram"] = a
        args.append(nc.dram_tensor(f"in_{name}_dram", a.shape, _mybir.dt.from_np(a.dtype), kind="ExternalInput").ap())
    shape = arrays["in_x_dram"].shape
    args.append(nc.dram_tensor("out_0_dram", shape, _mybir.dt.float32, kind="ExternalOutput").ap())
    cond_resid_kernel(nc, *args)
    r = _run(nc, [arrays], core_ids=[0])
    return r.results[0]["out_0_dram"]
```

```python
import math
from contextlib import ExitStack

import numpy as np
import concourse.bass as bass
from concourse import mybir

F32 = mybir.dt.float32
F16 = mybir.dt.float16
I32 = mybir.dt.int32
U32 = mybir.dt.uint32
ALU = mybir.AluOpType
ACT = mybir.ActivationFunctionType

P = 128
WARM = 18
GATHER = 8
WS = 64.0
PARTS_USED = [(0, 0), (1, 0), (0, 1)]

TWO_PI = 2.0 * math.pi
PI_DOWN = 3.1415925


def cut(value, bits):
    m, e = math.frexp(value)
    return math.ldexp(math.floor(math.ldexp(m, bits)), e - bits)


PI_HI = cut(TWO_PI, 12)
PI_LO = TWO_PI - PI_HI
LN2_HI = cut(math.log(2.0), 12)
LN2_LO = math.log(2.0) - LN2_HI
EXP_TERMS = 7


def cond_resid_kernel(nc, x, cond, slot, lang, length, W0, W1, b1, lora_A, lora_B,
                      W2, Wr, A2, B2, log_dt, C, log_A_real, A_imag, D, out):
    NB, NH, T = x.shape
    KC = T // P
    R = lora_A.shape[2]
    E = Wr.shape[0]
    N = A_imag.shape[1]
    NTOK = NB * NH
    G0 = P // NH
    NG0 = NB // G0
    GA = P // R
    NGA = NB // GA
    TA = GA * NH
    NT = NTOK // P
    HT = P // NB
    HALF = NTOK // 2
    LB = 32
    LA = T // LB
    NL = LB + LA
    NTAB = NH * NL
    AW = E * R + E
    KPAD = T + P
    assert 2 * N == P and E * R == P and T == KC * P and E == 8

    kern_dram = nc.dram_tensor("conv_kernels", [NH * 2, KPAD], F16)

    with ExitStack() as ctx:
        def sb(name, shape, dt=F32):
            return ctx.enter_context(nc.sbuf_tensor(name, shape, dt))

        def sem(name):
            return ctx.enter_context(nc.semaphore(name))

        ident = sb("ident", [P, P])
        w0_mask = sb("w0_mask", [P, G0])
        lora_mask = sb("lora_mask", [P, GA])
        half_mask = sb("half_mask", [P, G0])
        steps = sb("steps", [P, T])
        powers_i = sb("powers_i", [P, NL], I32)
        powers = sb("powers", [P, NL])
        ids_i = sb("ids_i", [NB, 2], I32)
        ids = sb("ids", [P, 2])
        cond_bc = sb("cond_bc", [P, NB], I32)
        slot_bc = sb("slot_bc", [P, NB], I32)
        cond_own = sb("cond_own", [P, NG0, G0])
        slot_own = sb("slot_own", [P, NGA, GA])
        cond_sum = sb("cond_sum", [P, NG0])
        slot_sum = sb("slot_sum", [P, NGA])
        lane = sb("lane", [P, 1], I32)
        lane_mod = sb("lane_mod", [P, 2], I32)
        w0_index = sb("w0_index", [P, NG0], U32)
        lb_index = sb("lb_index", [P, NGA], U32)
        half_pi = sb("half_pi", [P, 1])
        conv_mask = sb("conv_mask", [P, T])
        steps_i = conv_mask[:, :].bitcast(I32)
        lang_bias = sb("lang_bias", [P, E])
        bias_sb = sb("bias_sb", [P, KC])

        x_sb = sb("x_sb", [P, NG0, T])
        w0_blocks = sb("w0_blocks", [P, NG0, NH])
        w0_diag = sb("w0_diag", [P, NG0, P])
        gh16 = sb("gh16", [P, 2, NT, P], F16)
        w1t = sb("w1t", [P, 2, KC, T], F16)
        w2t = sb("w2t", [P, 2, KC, T], F16)
        awt = sb("awt", [P, 2, KC, AW], F16)
        b2t = sb("b2t", [P, 2, T], F16)
        la16 = sb("la16", [P, 2, KC, NB, R], F16)
        lb16 = sb("lb16", [P, 2, NGA, T], F16)
        xt16 = sb("xt16", [P, 2, KC, NTOK], F16)
        lora_h = sb("lora_h", [P, NGA, P])
        lora_h16 = sb("lora_h16", [P, 2, NGA, TA], F16)
        x2_sb = sb("x2_sb", [P, 2, NH, NB // 2])
        x2t16 = sb("x2t16", [P, 2, KC, NH, NB], F16)
        toep = sb("toep", [P, NH, 2, T], F16)
        zeros16 = sb("zeros16", [2 * NH, P], F16)

        arena = sb("arena", [P, KC * T + NB * KC * R + NGA * T])
        wide = [arena[:, 0:KC * T], arena[:, KC * T:KC * T + NB * KC * R], arena[:, KC * T + NB * KC * R:]]
        w1_nat = wide[0].rearrange("p (k i) -> p k i", k=KC)
        w2_nat = w1_nat
        out_sb = wide[0].rearrange("p (k i) -> p k i", i=T)
        la_sb = wide[1].rearrange("p (b j) -> p b j", b=NB)
        lb_sb = wide[2].rearrange("p (g o) -> p g o", g=NGA)

        toep_flat = toep[:, :, :, :].rearrange("p h c t -> p (h c t)").bitcast(F32)

        def table(i):
            return toep_flat[:, i * NTAB:(i + 1) * NTAB].rearrange("p (h l) -> p h l", h=NH)

        tab_th, tab_abs, tab_mag = table(0), table(1), table(2)
        tab_ki = table(3).bitcast(I32)

        K0 = 4 * NTAB
        trig_b = toep_flat[:, K0:K0 + NH * LB].rearrange("p (h b) -> p h b", h=NH)
        K0 += NH * LB
        cos_a = toep_flat[:, K0:K0 + NH * LA].rearrange("p (h a) -> p h a", h=NH)
        K0 += NH * LA
        sin_a = toep_flat[:, K0:K0 + NH * LA].rearrange("p (h a) -> p h a", h=NH)
        K0 += NH * LA
        k64 = toep_flat[0:LA, K0:K0 + NH * LB].rearrange("a (h b) -> a h b", h=NH)
        K0 += NH * LB
        k16 = toep_flat[0:LA, K0:K0 + NH * LB].bitcast(F16).rearrange("a (h c b) -> a h c b", h=NH, c=2)

        early = w2t[:, :, :, :].rearrange("p c k o -> p (c k o)").bitcast(F32)
        x_flat = x_sb[:, :, :].rearrange("p g t -> p (g t)")
        a2_nat = x_flat[:, 0:T]
        wr_nat = x_flat[0:E, T:2 * T]
        b2_nat = x_flat[:, 2 * T:3 * T].rearrange("p (k e r) -> p k e r", k=KC, e=E)
        zcat = b2t[0:NH, :, :].rearrange("h c o -> h (c o)").bitcast(F32).rearrange("h (i c n) -> h i c n", i=4, c=2)
        SLOTS = 21
        small = early[0:NH, 0:SLOTS * (N + 1)].rearrange("h (i n) -> h i n", i=SLOTS)
        S0 = SLOTS * (N + 1)
        small_i = early[0:NH, S0:S0 + 3 * (N + 1)].bitcast(I32).rearrange("h (i n) -> h i n", i=3)
        S0 += 3 * (N + 1)
        b1_nat = early[0:KC, S0:S0 + P]

        sC = sb("sC", [NH, N, 2])
        sX = sb("sX", [NH, N + 1])
        sAi = sb("sAi", [NH, N])
        zt = sb("zt", [P, 4, NH])
        D_row = sb("D_row", [LA, NH])

        logit = sb("logit", [P, NT, E])
        top_v = sb("top_v", [P, NT, 8])
        top_i = sb("top_i", [P, NT, 8], U32)
        top_f = sb("top_f", [P, NT, 2])
        gdiff = sb("gdiff", [P, NT])
        gexp = sb("gexp", [P, NT])
        gsum = sb("gsum", [P, NT])
        grec = sb("grec", [P, NT])
        gw = sb("gw", [P, NT, 2])
        onehot = sb("onehot", [P, NT, 2, E])
        gates = sb("gates", [P, NT, E])
        gated_h = w0_diag
        conv_out = x2_sb[:, :, :, :].rearrange("p s h b -> p s (h b)")

        bank = [ctx.enter_context(nc.psum_tensor(f"bank{i}", [P, 512], F32)) for i in range(8)]

        full = [sem(f"psum_full{i}") for i in range(8)]
        free = [sem(f"psum_free{i}") for i in range(8)]
        unit = {}
        used = [0] * 8

        def add_unit(key, b):
            unit[key] = (b, used[b])
            used[b] += 1

        for k in range(KC):
            add_unit(("w1t", k), 4 + k)
        for g in range(NG0):
            add_unit(("l0", g), (0, 1, 2, 3, 4, 5, 6, 0)[g])
        add_unit(("z", 0), 1)
        for m in range(KC):
            add_unit(("l1", (m, 0)), (2, 3, 0, 1)[m])
        add_unit(("l1", (0, 1)), 6)
        for i in range(NGA // 2):
            add_unit(("la", i), 4 + i)
        add_unit(("l1", (1, 1)), 7)
        add_unit(("w2t", 0), 5)
        add_unit(("w2t", 1), 4)
        add_unit(("l1", (2, 1)), 2)
        add_unit(("z", 1), 6)
        add_unit(("a2t", 0), 3)
        add_unit(("wrt", 0), 0)
        add_unit(("l1", (3, 1)), 1)
        add_unit(("k", 0), 2)
        add_unit(("k", 1), 4)
        add_unit(("w2t", 2), 6)
        add_unit(("w2t", 3), 3)
        add_unit(("b2t", 0), 0)
        l1_order = [(m, n) for n in range(2) for m in range(KC)]
        for i in range(NT // 2):
            add_unit(("aw", i), (7, 6, 4, 5)[i])
        for t in range(NT):
            add_unit(("l2", t), (2, 1, 3, 0)[t % 4])
            add_unit(("x3t", t), 6)
            if t < NT - 1:
                add_unit(("conv", t), 4 + t % 2)
        for i in range(NT // 2):
            add_unit(("gt", i), 7)
        add_unit(("conv", (NT - 1, 0)), 7)
        add_unit(("conv", (NT - 1, 1)), 4 + (NT - 1) % 2)

        turn_step = [1] + [2 * i for i in range(1, NT // 2)]

        def ps(key):
            return bank[unit[key][0]]

        def claim(eng, key):
            b, n = unit[key]
            if n:
                eng.wait_ge(free[b], n)

        def await_unit(eng, key):
            b, n = unit[key]
            eng.wait_ge(full[b], n + 1)

        def await_read(eng, key):
            b, n = unit[key]
            eng.wait_ge(free[b], n + 1)

        def full_of(key):
            return full[unit[key][0]]

        def free_of(key):
            return free[unit[key][0]]

        ids_in = sem("ids_in")
        cond_in = sem("cond_in")
        slot_in = sem("slot_in")
        x_in = [sem(f"x_in{g}") for g in range(NG0)]
        w1_in = sem("w1_in")
        w2_in = sem("w2_in")
        a2_in = sem("a2_in")
        b1_in = sem("b1_in")
        b2_in = sem("b2_in")
        bias_ready = sem("bias_ready")
        s4_in = sem("s4_in")
        ai_in = sem("ai_in")
        c_in = sem("c_in")
        d_in = sem("d_in")
        la_in = [sem(f"la_in{j}") for j in range(NGA)]
        w0_in = [sem(f"w0_in{g}") for g in range(NG0)]
        lb_in = [sem(f"lb_in{j}") for j in range(NGA)]
        lane_ready = sem("lane_ready")
        steps_ready = sem("steps_ready")
        w0_index_ready = sem("w0_index_ready")
        lb_index_ready = sem("lb_index_ready")
        lora_zeroed = sem("lora_zeroed")
        ids_ready = sem("ids_ready")
        consts = sem("consts")
        pool_chain = sem("pool_chain")
        chain = sem("dve_chain")
        eye_added1 = sem("eye_added1")
        eye_added2 = sem("eye_added2")
        w0_zeroed = sem("w0_zeroed")
        w0_ready = sem("w0_ready")
        w1t_hi = sem("w1t_hi")
        half_angle = sem("half_angle")
        half_trig = sem("half_trig")
        rates_ready = sem("rates_ready")
        z_ready = sem("z_ready")
        x1_hi = sem("x1_hi")
        la_scaled = sem("la_scaled")
        la_hi = sem("la_hi")
        la_ready = sem("la_ready")
        lb_scaled = sem("lb_scaled")
        lb_hi = sem("lb_hi")
        lb_ready = sem("lb_ready")
        half_mask_ready = sem("half_mask_ready")
        lh_hi = sem("lh_hi")
        lh_ready = sem("lh_ready")
        decay_ready = sem("decay_ready")
        mag_ready = sem("mag_ready")
        angle_ready = sem("angle_ready")
        trig_ready = sem("trig_ready")
        pq_ready = sem("pq_ready")
        d_added = sem("d_added")
        k_hi = sem("k_hi")
        k_ready = sem("k_ready")
        k_put = sem("k_put")
        zeros_put = sem("zeros_put")
        toep_in = [sem(f"toep_in{g}") for g in range(NT)]
        w2_hi = sem("w2_hi")
        a2_hi = sem("a2_hi")
        b2_hi = sem("b2_hi")
        x2_hi = sem("x2_hi")
        x2_ready = sem("x2_ready")
        x2_last = sem("x2_last")
        gap_ready = sem("gap_ready")
        gexp_ready = sem("gexp_ready")
        gt_hi = sem("gt_hi")
        x3t_hi = sem("x3t_hi")
        out_ready = sem("out_ready")
        last_ready = sem("last_ready")
        out_put = [sem(f"out_put{i}") for i in range(5)]

        block = ctx.enter_context(nc.Block())
        kern_rows = kern_dram.ap()

        def out_rows(t, c0, c1):
            return bass.AP(out.tensor, t * HT * T + c0, [[T, HT], [NH * T, NB], [1, c1 - c0]])

        @block.sync
        def _(sp):
            sp.dma_start(cond_bc[:, :], bass.AP(cond.tensor, 0, [[0, P], [1, NB]])).then_inc(cond_in, 16)
            sp.dma_start(slot_bc[:, :], bass.AP(slot.tensor, 0, [[0, P], [1, NB]])).then_inc(slot_in, 16)

            def load_x(g):
                sp.dma_start(x_sb[:, g, :], x[g * G0:(g + 1) * G0].rearrange("b c t -> (b c) t")).then_inc(x_in[g], 16)

            sp.dma_start(w1_nat[:, :, :], W1.rearrange("(k p) i -> p k i", p=P)).then_inc(w1_in, 16)
            for g in range(2):
                load_x(g)
            sp.wait_ge(slot_in, 16)
            for b0 in range(0, NB, GATHER):
                regs = [sp.alloc_register(f"slot{b0 + i}") for i in range(GATHER)]
                sp.load(regs, slot_bc[0:1, b0:b0 + GATHER])
                for i, reg in enumerate(regs):
                    row = sp.snap(reg, min_val=0, max_val=lora_A.shape[0] - 1)
                    sp.dma_start(la_sb[:, b0 + i, :],
                                 lora_A[bass.ds(row, 1)].rearrange("s (p k) r -> p (s k r)", p=P)).then_inc(
                                     la_in[(b0 + i) // GA], 16)
                    if b0 + i + 2 < NG0:
                        load_x(b0 + i + 2)
            for k in range(KC):
                await_unit(sp, ("w1t", k))
            sp.dma_start(w2_nat[:, :, :], W2.rearrange("(k p) i -> p k i", p=P)).then_inc(w2_in, 16)
            for g in range(NG0):
                await_unit(sp, ("l0", g))
            sp.dma_start(a2_nat, A2.rearrange("e r i -> (e r) i")).then_inc(a2_in, 16)
            sp.dma_start(wr_nat, Wr).then_inc(a2_in, 16)
            for k in range(KC):
                sp.dma_start(b2_nat[:, k], B2[:, k * P:(k + 1) * P, :].rearrange("e p r -> p e r")).then_inc(b2_in, 16)
            sp.dma_start(D_row[:, :], bass.AP(D.tensor, 0, [[0, LA], [1, NH]])).then_inc(d_in, 16)
            sp.dma_start(ids_i[:, 0:1], lang.rearrange("(b a) -> b a", a=1)).then_inc(ids_in, 16)
            sp.dma_start(ids_i[:, 1:2], length.rearrange("(b a) -> b a", a=1)).then_inc(ids_in, 16)
            sp.wait_ge(k_ready, 1)
            sp.dma_start(kern_rows[:, 0:T].rearrange("(h c) (a b) -> a (h c) b", c=2, b=LB),
                         k16[:, :, :, :].rearrange("a h c b -> a (h c) b")).then_inc(k_put, 16)
            sp.wait_ge(k_put, 16)
            sp.wait_ge(zeros_put, 16)
            for g in range(NT):
                rows = 2 * HT
                src = bass.AP(kern_rows.tensor, g * rows * KPAD, [[1, P], [KPAD, rows], [1, T]])
                sp.dma_start(toep[:, g * HT:(g + 1) * HT, :, :].rearrange("p h c t -> p (h c) t"),
                             src).then_inc(toep_in[g], 16)
            for t in range(NT - 1):
                sp.wait_ge(out_ready, t + 1)
                sp.dma_start(out_rows(t, 0, T), out_sb[:, t % 4, :]).then_inc(out_put[t % 4], 16)
            sp.wait_ge(out_ready, NT)
            sp.dma_start(out_rows(NT - 1, 0, T // 2), out_sb[:, (NT - 1) % 4, 0:T // 2]).then_inc(out_put[4], 16)
            sp.wait_ge(last_ready, 1)
            sp.dma_start(out_rows(NT - 1, T // 2, T), out_sb[:, (NT - 1) % 4, T // 2:T]).then_inc(out_put[4], 16)
            for i in range(4):
                sp.wait_ge(out_put[i], 16 * len(range(i, NT - 1, 4)))
            sp.wait_ge(out_put[4], 16 * 2)

        @block.gpsimd
        def _(pool):
            count = [0]

            def link(ins):
                count[0] += 1
                ins.then_inc(pool_chain, 1)
                pool.wait_ge(pool_chain, count[0])

            nc.gpsimd.iota(lane[:, :], pattern=[[0, 1]], base=0, channel_multiplier=1).then_inc(lane_ready, 1)
            for mask, blocks, rows, value in ((w0_mask, G0, NH, 1.0), (lora_mask, GA, R, 2.0 / WS)):
                link(nc.gpsimd.memset(mask[:, :], value))
                link(nc.gpsimd.affine_select(out=mask[:, :], in_=mask[:, :], compare_op=ALU.is_ge, fill=0.0, base=0,
                                             pattern=[[-rows, blocks]], channel_multiplier=1))
                nc.gpsimd.affine_select(out=mask[:, :], in_=mask[:, :], compare_op=ALU.is_ge, fill=0.0,
                                        base=rows - 1, pattern=[[rows, blocks]],
                                        channel_multiplier=-1).then_inc(consts, 1)
            link(nc.gpsimd.memset(ident[:, :], 0.0))
            nc.gpsimd.affine_select(out=ident[:, :], in_=ident[:, :], compare_op=ALU.not_equal, fill=1.0, base=0,
                                    pattern=[[-1, P]], channel_multiplier=1).then_inc(consts, 1)
            W0_rows = W0.rearrange("s c d -> (s c) d")
            pool.wait_ge(w0_index_ready, 1)
            for g in range(NG0):
                pool.indirect_dma_start(out=w0_blocks[:, g, :], out_offset=None, in_=W0_rows,
                                        in_offset=bass.IndirectOffsetOnAxis(w0_index[:, g:g + 1], 0)).then_inc(w0_in[g], 16)
            nc.gpsimd.iota(powers_i[:, 0:LB], pattern=[[-1, LB]], base=LB - 1, channel_multiplier=0).then_inc(steps_ready, 1)
            nc.gpsimd.iota(powers_i[:, LB:NL], pattern=[[-LB, LA]], base=T - LB, channel_multiplier=0).then_inc(steps_ready, 1)
            pool.wait_ge(steps_ready, 2)
            nc.gpsimd.tensor_copy(powers[:, :], powers_i[:, :]).then_inc(steps_ready, 1)
            lb_rows = lora_B.rearrange("s r o -> (s r) o")
            pool.wait_ge(lb_index_ready, 1)
            for j in range(NGA):
                pool.indirect_dma_start(out=lb_sb[:, j, :], out_offset=None, in_=lb_rows,
                                        in_offset=bass.IndirectOffsetOnAxis(lb_index[:, j:j + 1], 0)).then_inc(lb_in[j], 16)
            pool.wait_ge(steps_ready, 3)
            await_read(pool, ("z", 0))
            nc.gpsimd.tensor_tensor(tab_th, zt[:, 1, :].unsqueeze(2).to_broadcast([P, NH, NL]),
                                    powers[:, :].unsqueeze(1).to_broadcast([P, NH, NL]), ALU.mult).then_inc(decay_ready, 1)
            nc.gpsimd.tensor_tensor(tab_mag, zt[:, 0, :].unsqueeze(2).to_broadcast([P, NH, NL]),
                                    powers[:, :].unsqueeze(1).to_broadcast([P, NH, NL]), ALU.mult).then_inc(decay_ready, 1)
            def la_low(j):
                pool.wait_ge(la_hi, j + 1)
                B = slice(j * GA, (j + 1) * GA)
                nc.gpsimd.tensor_tensor(la16[:, 1, :, B], la_sb[:, B, :].rearrange("p b (k r) -> p k b r", k=KC),
                                        la16[:, 0, :, B], ALU.subtract).then_inc(la_ready, 1)

            la_low(0)
            nc.gpsimd.iota(steps_i, pattern=[[1, T]], base=0, channel_multiplier=0).then_inc(steps_ready, 1)
            link(nc.gpsimd.memset(zeros16[:, :], 0.0))
            pool.dma_start(kern_rows[:, T:], zeros16[:, :]).then_inc(zeros_put, 16)
            for j in range(1, NGA):
                la_low(j)
            for j in range(NGA):
                pool.wait_ge(lb_hi, j + 1)
                nc.gpsimd.tensor_tensor(lb16[:, 1, j, :], lb_sb[:, j, :], lb16[:, 0, j, :],
                                        ALU.subtract).then_inc(lb_ready, 1)
            pool.wait_ge(w2_in, 16)
            for k in range(KC):
                d = w2_nat[:, k, k * P:(k + 1) * P]
                nc.gpsimd.tensor_tensor(d, d, ident[:, :], ALU.add).then_inc(eye_added2, 1)
            for i, (m, n) in enumerate(l1_order[:-1]):
                pool.wait_ge(x2_hi, i + 1)
                dst = x2t16[:, :, m, :, n * (NB // 2):(n + 1) * (NB // 2)]
                nc.gpsimd.tensor_tensor(dst[:, 1], x2_sb[:, i % 2], dst[:, 0], ALU.subtract).then_inc(x2_ready, 1)
            pool.wait_ge(d_in, 16)
            link(nc.gpsimd.tensor_scalar(D_row[:, :], D_row[:, :], ident[0:LA, LA - 1:LA], WS, ALU.mult, ALU.mult))
            await_read(pool, ("k", 0))
            await_read(pool, ("k", 1))
            nc.gpsimd.tensor_tensor(k64[:, :, LB - 1], k64[:, :, LB - 1], D_row[:, :], ALU.add).then_inc(d_added, 1)
            pool.wait_ge(k_hi, 1)
            nc.gpsimd.tensor_tensor(k16[:, :, 1, :], k64[:, :, :], k16[:, :, 0, :], ALU.subtract).then_inc(k_ready, 1)
            for t in range(NT):
                c = slice(0, T // 2 if t == NT - 1 else T)
                await_read(pool, ("conv", t if t < NT - 1 else (t, 0)))
                if t >= 4:
                    pool.wait_ge(out_put[t % 4], 16 * (t // 4))
                nc.gpsimd.tensor_tensor(out_sb[:, t % 4, c], conv_out[:, t % 2, c], x_sb[:, t, c],
                                        ALU.add).then_inc(out_ready, 1)

        @block.scalar
        def _(act):
            act.dma_start(sX[:, 0:N], log_A_real).then_inc(s4_in, 16)
            act.dma_start(sX[:, N:N + 1], log_dt.rearrange("(h a) -> h a", a=1)).then_inc(s4_in, 16)
            act.dma_start(sAi[:, :], A_imag).then_inc(ai_in, 16)
            act.dma_start(sC[:, :, :], C).then_inc(c_in, 16)
            act.dma_start(b1_nat, b1.rearrange("(k p) -> k p", p=P)).then_inc(b1_in, 16)

            for k in range(KC):
                await_unit(act, ("w1t", k))
                nc.scalar.activation(w1t[:, 0, k, :], ps(("w1t", k))[:, :], ACT.Copy, scale=WS).then_inc(w1t_hi, 1)
            def x1_high(g):
                await_unit(act, ("l0", g))
                nc.scalar.activation(xt16[:, 0, :, g * P:(g + 1) * P],
                                     ps(("l0", g))[:, :].rearrange("p (k n) -> p k n", k=KC), ACT.Copy).then_inc(x1_hi, 1)

            for g in range(NG0):
                x1_high(g)

            def la_high(j):
                act.wait_ge(la_in[j], 16 * GA)
                B = slice(j * GA, (j + 1) * GA)
                nc.scalar.activation(la_sb[:, B, :], la_sb[:, B, :], ACT.Copy, scale=WS).then_inc(la_scaled, 1)
                act.wait_ge(la_scaled, j + 1)
                nc.scalar.activation(la16[:, 0, :, B], la_sb[:, B, :].rearrange("p b (k r) -> p k b r", k=KC),
                                     ACT.Copy).then_inc(la_hi, 1)

            def lb_high(j):
                act.wait_ge(lb_in[j], 16)
                nc.scalar.activation(lb_sb[:, j, :], lb_sb[:, j, :], ACT.Copy, scale=WS).then_inc(lb_scaled, 1)
                act.wait_ge(lb_scaled, j + 1)
                nc.scalar.activation(lb16[:, 0, j, :], lb_sb[:, j, :], ACT.Copy).then_inc(lb_hi, 1)

            la_high(0)
            for j in range(NGA):
                lb_high(j)
            act.wait_ge(decay_ready, 2)
            nc.scalar.activation(tab_mag, tab_mag, ACT.Exp).then_inc(mag_ready, 1)
            la_high(1)
            act.wait_ge(half_angle, 2)
            nc.scalar.activation(small[:, 10, 0:N], small[:, 8, 0:N], ACT.Sin).then_inc(half_trig, 1)
            nc.scalar.activation(small[:, 11, 0:N], small[:, 9, 0:N], ACT.Sin).then_inc(half_trig, 1)
            la_high(2)
            la_high(3)
            act.wait_ge(angle_ready, 2)
            nc.scalar.activation(trig_b[0:N], tab_abs[0:N, :, 0:LB], ACT.Sin, bias=half_pi[0:N, :],
                                 scale=-1.0).then_inc(trig_ready, 1)
            nc.scalar.activation(trig_b[N:P], tab_th[N:P, :, 0:LB], ACT.Sin).then_inc(trig_ready, 1)
            nc.scalar.activation(cos_a, tab_abs[:, :, LB:NL], ACT.Sin, bias=half_pi[:, :],
                                 scale=-1.0).then_inc(trig_ready, 1)
            nc.scalar.activation(sin_a, tab_th[:, :, LB:NL], ACT.Sin).then_inc(trig_ready, 1)
            for i in range(NGA // 2):
                J = slice(2 * i, 2 * i + 2)
                await_read(act, ("la", i))
                for q in range(2):
                    rows = slice(q * N, (q + 1) * N)
                    ins = nc.scalar.activation(lora_h16[rows, 0, J, q * P:(q + 1) * P], lora_h[rows, J, :], ACT.Copy)
                ins.then_inc(lh_hi, 1)

            def w2t_high(k):
                await_unit(act, ("w2t", k))
                nc.scalar.activation(w2t[:, 0, k, :], ps(("w2t", k))[:, :], ACT.Copy, scale=WS).then_inc(w2_hi, 1)

            def a2_high():
                await_unit(act, ("a2t", 0))
                nc.scalar.activation(awt[:, 0, :, 0:P], ps(("a2t", 0))[:, :].rearrange("p (k n) -> p k n", k=KC),
                                     ACT.Copy, scale=WS).then_inc(a2_hi, 1)
                await_unit(act, ("wrt", 0))
                nc.scalar.activation(awt[:, 0, :, P:AW], ps(("wrt", 0))[:, 0:KC * E].rearrange("p (k n) -> p k n", k=KC),
                                     ACT.Copy, scale=WS).then_inc(a2_hi, 1)

            def b2_high():
                await_unit(act, ("b2t", 0))
                nc.scalar.activation(b2t[:, 0, :], ps(("b2t", 0))[:, :], ACT.Copy, scale=WS).then_inc(b2_hi, 1)

            act.wait_ge(bias_ready, 1)
            for i, (m, n) in enumerate(l1_order):
                await_unit(act, ("l1", (m, n)))
                if i >= 2:
                    act.wait_ge(x2_ready, i - 1)
                nc.scalar.activation(x2_sb[:, i % 2], ps(("l1", (m, n)))[:, :].rearrange("p (b h) -> p h b", h=NH),
                                     ACT.Identity, bias=bias_sb[:, m:m + 1],
                                     scale=1.0 / WS).then_inc(free_of(("l1", (m, n))), 1)
                await_read(act, ("l1", (m, n)))
                nc.scalar.activation(x2t16[:, 0, m, :, n * (NB // 2):(n + 1) * (NB // 2)], x2_sb[:, i % 2],
                                     ACT.Copy).then_inc(x2_hi, 1)
                if (m, n) == (1, 1):
                    act.wait_ge(z_ready, 5)
                    w2t_high(0)
                    w2t_high(1)
                if (m, n) == (2, 1):
                    a2_high()
            w2t_high(2)
            w2t_high(3)
            b2_high()
            HH = NH // 2
            for s in range(2):
                await_unit(act, ("k", s))
                nc.scalar.activation(k64[:, s * HH:(s + 1) * HH, :].rearrange("a h b -> a (h b)"), ps(("k", s))[0:LA, :],
                                     ACT.Copy, scale=WS).then_inc(free_of(("k", s)), 1)
            act.wait_ge(d_added, 1)
            nc.scalar.activation(k16[:, :, 0, :], k64[:, :, :], ACT.Copy).then_inc(k_hi, 1)
            for s in range(2):
                act.wait_ge(gap_ready, s + 1)
                nc.scalar.activation(gexp[:, s * 4:s * 4 + 4], gdiff[:, s * 4:s * 4 + 4], ACT.Exp).then_inc(gexp_ready, 1)


            def gh_high(i):
                await_unit(act, ("gt", i))
                nc.scalar.activation(gh16[:, 0, 2 * i:2 * i + 2, :],
                                     ps(("gt", i))[:, 0:2 * P].rearrange("p (t n) -> p t n", t=2), ACT.Copy).then_inc(gt_hi, 1)

            def x3_sum(t):
                await_unit(act, ("l2", t))
                nc.scalar.activation(x_sb[:, t, :], ps(("l2", t))[:, :], ACT.Copy, scale=1.0 / WS).then_inc(free_of(("l2", t)), 1)

            def x3t_high(t):
                await_unit(act, ("x3t", t))
                nc.scalar.activation(xt16[:, 0, :, t * P:(t + 1) * P],
                                     ps(("x3t", t))[:, :].rearrange("p (k n) -> p k n", k=KC), ACT.Copy).then_inc(x3t_hi, 1)

            for i in range(1, NT + 2):
                if i in turn_step:
                    gh_high(turn_step.index(i))
                if i <= NT:
                    x3_sum(i - 1)
                if i >= 2:
                    x3t_high(i - 2)

        @block.vector
        def _(dve):
            count = [0]
            V = nc.vector

            def link(ins):
                count[0] += 1
                ins.then_inc(chain, 1)
                dve.wait_ge(chain, count[0])

            def exp_parts(src, w, slot0, islot):
                ki, p2 = small_i[:, islot, 0:w], small_i[:, islot + 1, 0:w]
                r, q = small[:, slot0, 0:w], small[:, slot0 + 1, 0:w]
                link(V.tensor_scalar(ki, src, 1.0 / math.log(2.0), None, ALU.mult))
                link(V.scalar_tensor_tensor(r, ki, -LN2_HI, src, ALU.mult, ALU.add))
                link(V.scalar_tensor_tensor(r, ki, -LN2_LO, r, ALU.mult, ALU.add))
                link(V.tensor_scalar(q, r, 1.0 / math.factorial(EXP_TERMS), None, ALU.mult))
                for n in range(EXP_TERMS - 1, 0, -1):
                    link(V.scalar_tensor_tensor(q, q, 1.0 / math.factorial(n), r, ALU.add, ALU.mult))
                link(V.tensor_scalar(p2, ki, 127.0, 0.0, ALU.add, ALU.max))
                link(V.tensor_scalar(p2, p2, 23, None, ALU.logical_shift_left))
                return q, p2.bitcast(F32)

            def reduce_angle(th, ki):
                link(V.tensor_scalar(ki, th, 1.0 / TWO_PI, None, ALU.mult))
                for part in (PI_HI, PI_LO):
                    link(V.scalar_tensor_tensor(th, ki, -part, th, ALU.mult, ALU.add))
                link(V.tensor_scalar(th, th, PI_DOWN, -PI_DOWN, ALU.min, ALU.max))

            V.memset(half_pi[:, :], math.pi / 2)
            V.memset(lora_h16[:, :, :, :], 0.0).then_inc(lora_zeroed, 1)
            V.memset(w0_diag[:, :, :], 0.0).then_inc(w0_zeroed, 1)
            dve.wait_ge(cond_in, 16)
            dve.wait_ge(consts, 1)
            link(V.tensor_tensor(cond_own[:, :, :], cond_bc[:, :].rearrange("p (g b) -> p g b", g=NG0),
                                 w0_mask[:, :].unsqueeze(1).to_broadcast([P, NG0, G0]), ALU.mult))
            link(V.reduce_sum(cond_sum[:, :], cond_own[:, :, :], axis=mybir.AxisListType.X))
            dve.wait_ge(lane_ready, 1)
            link(V.tensor_scalar(lane_mod[:, 0:1], lane[:, :], NH - 1, None, ALU.bitwise_and))
            link(V.tensor_scalar(lane_mod[:, 1:2], lane[:, :], R - 1, None, ALU.bitwise_and))
            V.scalar_tensor_tensor(w0_index[:, :], cond_sum[:, :], float(NH), lane_mod[:, 0:1].to_broadcast([P, NG0]),
                                   ALU.mult, ALU.add).then_inc(w0_index_ready, 1)
            dve.wait_ge(slot_in, 16)
            dve.wait_ge(consts, 2)
            link(V.tensor_tensor(slot_own[:, :, :], slot_bc[:, :].rearrange("p (g b) -> p g b", g=NGA),
                                 lora_mask[:, :].unsqueeze(1).to_broadcast([P, NGA, GA]), ALU.mult))
            link(V.reduce_sum(slot_sum[:, :], slot_own[:, :, :], axis=mybir.AxisListType.X))
            V.scalar_tensor_tensor(lb_index[:, :], slot_sum[:, :], R * WS / 2.0, lane_mod[:, 1:2].to_broadcast([P, NGA]),
                                   ALU.mult, ALU.add).then_inc(lb_index_ready, 1)
            V.tensor_tensor(half_mask[:, :], lora_mask[:, 0:G0], lora_mask[:, G0:GA], ALU.add).then_inc(half_mask_ready, 1)

            def w0_blocks_of(g0, g1):
                for g in range(g0, g1):
                    dve.wait_ge(w0_in[g], 16)
                for b in range(G0):
                    own = slice(b * NH, (b + 1) * NH)
                    ins = V.tensor_tensor(w0_diag[own, g0:g1, own], w0_blocks[own, g0:g1, :],
                                          ident[own, own].unsqueeze(1).to_broadcast([NH, g1 - g0, NH]), ALU.add)
                ins.then_inc(w0_ready, g1 - g0)

            def w1_eye():
                dve.wait_ge(w1_in, 16)
                for k in range(KC):
                    d = w1_nat[:, k, k * P:(k + 1) * P]
                    V.tensor_tensor(d, d, ident[:, :], ALU.add).then_inc(eye_added1, 1)

            def w1t_low(k):
                dve.wait_ge(w1t_hi, k + 1)
                V.scalar_tensor_tensor(w1t[:, 1, k, :], ps(("w1t", k))[:, :], WS, w1t[:, 0, k, :],
                                       ALU.mult, ALU.subtract).then_inc(free_of(("w1t", k)), 1)

            def x1_low(g):
                dve.wait_ge(x1_hi, g + 1)
                V.tensor_tensor(xt16[:, 1, :, g * P:(g + 1) * P], ps(("l0", g))[:, :].rearrange("p (k n) -> p k n", k=KC),
                                xt16[:, 0, :, g * P:(g + 1) * P], ALU.subtract).then_inc(free_of(("l0", g)), 1)

            dve.wait_ge(s4_in, 16 * 2)
            q, p2 = exp_parts(sX[:, :], N + 1, 0, 0)
            rates = small[:, 2, :]
            link(V.scalar_tensor_tensor(rates, q, 1.0, p2, ALU.add, ALU.mult))
            rate, dt = small[:, 2, 0:N], small[:, 2, N:N + 1]
            dve.wait_ge(consts, 3)
            dve.wait_ge(w0_zeroed, 1)
            w1_eye()
            w0_blocks_of(0, 1)
            w0_blocks_of(1, 2)
            w1t_low(0)
            w0_blocks_of(2, 4)
            w1t_low(1)
            dve.wait_ge(ai_in, 16)
            dre, dim = small[:, 3, 0:N], small[:, 4, 0:N]
            V.tensor_scalar(dre, rate, dt, -1.0, ALU.mult, ALU.mult).then_inc(rates_ready, 1)
            V.tensor_scalar(dim, sAi[:, :], dt, None, ALU.mult).then_inc(rates_ready, 1)
            dve.wait_ge(rates_ready, 2)
            for half in range(2):
                V.tensor_copy(zcat[:, 0, half, :], dre).then_inc(z_ready, 1)
                V.tensor_copy(zcat[:, 1, half, :], dim).then_inc(z_ready, 1)
            w0_blocks_of(4, 6)
            x1_low(0)
            w1t_low(2)
            x1_low(1)
            w0_blocks_of(6, 8)
            x1_low(2)
            x1_low(3)
            w1t_low(3)
            await_unit(dve, ("z", 0))
            V.tensor_copy(bias_sb[:, :], ps(("z", 0))[:, 2 * NH:2 * NH + KC]).then_inc(bias_ready, 1)
            V.tensor_copy(zt[:, 0:2, :].rearrange("p a h -> p (a h)"), ps(("z", 0))[:, 0:2 * NH]).then_inc(free_of(("z", 0)), 1)
            for g in range(4, NG0):
                x1_low(g)
            ha, hc = small[:, 8, 0:N], small[:, 9, 0:N]
            link(V.tensor_scalar(ha, dim, 0.5, None, ALU.mult))
            reduce_angle(ha, small_i[:, 2, 0:N])
            link(V.tensor_scalar(hc, ha, -1.0, None, ALU.mult))
            link(V.tensor_tensor(hc, hc, ha, ALU.min))
            V.tensor_scalar(hc, hc, math.pi / 2, None, ALU.add).then_inc(half_angle, 2)
            dve.wait_ge(decay_ready, 1)
            reduce_angle(tab_th, tab_ki)
            V.scalar_tensor_tensor(tab_abs, tab_th, -1.0, tab_th, ALU.mult, ALU.max).then_inc(angle_ready, 2)
            q, p2 = exp_parts(dre, N, 5, 0)
            em1, e1 = small[:, 7, 0:N], small[:, 12, 0:N]
            link(V.tensor_scalar(e1, p2, -1.0, None, ALU.add))
            link(V.tensor_tensor(em1, q, p2, ALU.mult))
            link(V.tensor_tensor(em1, em1, e1, ALU.add))
            link(V.tensor_scalar(e1, em1, 1.0, None, ALU.add))
            dve.wait_ge(half_trig, 2)
            sn, cs = small[:, 10, 0:N], small[:, 11, 0:N]
            t0, t1, t2, er, ei = (small[:, i, 0:N] for i in (13, 14, 15, 16, 17))
            fr, fi, inv = (small[:, i, 0:N] for i in (18, 19, 20))
            link(V.tensor_tensor(t0, sn, sn, ALU.mult))
            link(V.tensor_tensor(t0, t0, e1, ALU.mult))
            link(V.scalar_tensor_tensor(er, t0, -2.0, em1, ALU.mult, ALU.add))
            link(V.tensor_tensor(t1, sn, cs, ALU.mult))
            link(V.scalar_tensor_tensor(ei, t1, 2.0, e1, ALU.mult, ALU.mult))
            dve.wait_ge(half_mask_ready, 1)
            dve.wait_ge(lora_zeroed, 1)

            def lora_masked(i):
                await_unit(dve, ("la", i))
                J = slice(2 * i, 2 * i + 2)
                V.tensor_tensor(lora_h[:, J, :].rearrange("p j (b h) -> p j b h", b=G0),
                                ps(("la", i))[:, 0:2 * P].rearrange("p (j b h) -> p j b h", j=2, b=G0),
                                half_mask[:, :].unsqueeze(1).unsqueeze(3).to_broadcast([P, 2, G0, NH]),
                                ALU.mult).then_inc(free_of(("la", i)), 1)

            def lora_low(i):
                dve.wait_ge(lh_hi, i + 1)
                J = slice(2 * i, 2 * i + 2)
                for q in range(2):
                    rows, own = slice(q * N, (q + 1) * N), slice(q * P, (q + 1) * P)
                    ins = V.tensor_tensor(lora_h16[rows, 1, J, own], lora_h[rows, J, :], lora_h16[rows, 0, J, own],
                                          ALU.subtract)
                ins.then_inc(lh_ready, 1)

            lora_masked(0)
            lora_masked(1)
            lora_low(0)
            lora_low(1)
            link(V.tensor_tensor(t0, rate, rate, ALU.mult))
            link(V.tensor_tensor(t1, sAi[:, :], sAi[:, :], ALU.mult))
            link(V.tensor_tensor(t0, t0, t1, ALU.add))
            link(V.reciprocal(inv, t0))
            link(V.scalar_tensor_tensor(t0, er, -1.0, rate, ALU.mult, ALU.mult))
            link(V.tensor_tensor(t1, ei, sAi[:, :], ALU.mult))
            link(V.tensor_tensor(fr, t0, t1, ALU.add))
            link(V.scalar_tensor_tensor(t0, ei, -1.0, rate, ALU.mult, ALU.mult))
            link(V.tensor_tensor(t1, er, sAi[:, :], ALU.mult))
            link(V.tensor_tensor(fi, t0, t1, ALU.subtract))
            link(V.scalar_tensor_tensor(fr, fr, 2.0, inv, ALU.mult, ALU.mult))
            link(V.scalar_tensor_tensor(fi, fi, 2.0, inv, ALU.mult, ALU.mult))
            dve.wait_ge(c_in, 16)
            cr, ci = sC[:, :, 0], sC[:, :, 1]
            link(V.tensor_tensor(t0, cr, fr, ALU.mult))
            link(V.tensor_tensor(t1, ci, fi, ALU.mult))
            link(V.tensor_tensor(zcat[:, 2, 0, :], t0, t1, ALU.subtract))
            link(V.tensor_tensor(t2, cr, fi, ALU.mult))
            link(V.tensor_tensor(t0, ci, fr, ALU.mult))
            link(V.scalar_tensor_tensor(zcat[:, 2, 1, :], t2, -1.0, t0, ALU.mult, ALU.subtract))
            link(V.tensor_copy(zcat[:, 3, 0, :], zcat[:, 2, 1, :]))
            V.tensor_scalar(zcat[:, 3, 1, :], zcat[:, 2, 0, :], -1.0, None, ALU.mult).then_inc(z_ready, 1)
            dve.wait_ge(mag_ready, 1)
            dve.wait_ge(trig_ready, 4)
            V.tensor_tensor(trig_b, trig_b, tab_mag[:, :, 0:LB], ALU.mult).then_inc(pq_ready, 1)
            dve.wait_ge(ids_in, 16 * 2)
            dve.wait_ge(steps_ready, 4)
            for q in range(HT):
                V.tensor_copy(ids[q * NB:(q + 1) * NB, :], ids_i[:, :]).then_inc(ids_ready, 1)
            link(V.tensor_copy(steps[:, :], steps_i))
            dve.wait_ge(ids_ready, HT)
            V.tensor_scalar(conv_mask[:, :], steps[:, :], ids[:, 1:2], 1.0 / WS, ALU.is_lt, ALU.mult)
            V.tensor_scalar(lang_bias[:, :], steps[:, 0:E], ids[:, 0:1], 5.0, ALU.is_equal, ALU.mult)
            await_unit(dve, ("z", 1))
            V.tensor_copy(zt[:, 2:4, :].rearrange("p a h -> p (a h)"), ps(("z", 1))[:, 0:2 * NH]).then_inc(free_of(("z", 1)), 1)
            await_read(dve, ("z", 1))
            link(V.tensor_tensor(cos_a, cos_a,
                                 zt[:, 2, :].unsqueeze(2).to_broadcast([P, NH, LA]), ALU.mult))
            link(V.tensor_tensor(sin_a, sin_a,
                                 zt[:, 3, :].unsqueeze(2).to_broadcast([P, NH, LA]), ALU.mult))
            link(V.tensor_tensor(cos_a, cos_a, sin_a, ALU.add))
            V.tensor_tensor(cos_a, cos_a, tab_mag[:, :, LB:NL], ALU.mult).then_inc(pq_ready, 1)
            def w2t_low(k):
                dve.wait_ge(w2_hi, k + 1)
                V.scalar_tensor_tensor(w2t[:, 1, k, :], ps(("w2t", k))[:, :], WS, w2t[:, 0, k, :],
                                       ALU.mult, ALU.subtract).then_inc(free_of(("w2t", k)), 1)

            dve.wait_ge(a2_hi, 1)
            V.scalar_tensor_tensor(awt[:, 1, :, 0:P], ps(("a2t", 0))[:, :].rearrange("p (k n) -> p k n", k=KC), WS,
                                   awt[:, 0, :, 0:P], ALU.mult, ALU.subtract).then_inc(free_of(("a2t", 0)), 1)
            dve.wait_ge(a2_hi, 2)
            V.scalar_tensor_tensor(awt[:, 1, :, P:AW], ps(("wrt", 0))[:, 0:KC * E].rearrange("p (k n) -> p k n", k=KC), WS,
                                   awt[:, 0, :, P:AW], ALU.mult, ALU.subtract).then_inc(free_of(("wrt", 0)), 1)
            w2t_low(0)
            w2t_low(1)
            last_m, last_n = l1_order[-1]
            dve.wait_ge(x2_hi, len(l1_order))
            dst = x2t16[:, :, last_m, :, last_n * (NB // 2):(last_n + 1) * (NB // 2)]
            V.tensor_tensor(dst[:, 1], x2_sb[:, (len(l1_order) - 1) % 2], dst[:, 0], ALU.subtract).then_inc(x2_last, 1)
            w2t_low(2)
            w2t_low(3)
            dve.wait_ge(b2_hi, 1)
            V.scalar_tensor_tensor(b2t[:, 1, :], ps(("b2t", 0))[:, :], WS, b2t[:, 0, :],
                                   ALU.mult, ALU.subtract).then_inc(free_of(("b2t", 0)), 1)

            def logits(t):
                await_unit(dve, ("aw", t // 2))
                at = (t % 2) * AW
                link(V.scalar_tensor_tensor(logit[:, t, :], ps(("aw", t // 2))[:, at + P:at + AW], 1.0 / WS,
                                            lang_bias[:, :], ALU.mult, ALU.add))
                link(V.max(top_v[:, t, :], logit[:, t, :]))
                link(V.max_index(top_i[:, t, :], top_v[:, t, :], logit[:, t, :]))

            for s in range(2):
                S = slice(s * 4, s * 4 + 4)
                for t in range(s * 4, s * 4 + 4):
                    logits(t)
                V.tensor_tensor(gdiff[:, S], top_v[:, S, 1], top_v[:, S, 0], ALU.subtract).then_inc(gap_ready, 1)
                link(V.tensor_copy(top_f[:, S, :], top_i[:, S, 0:2]))
                link(V.tensor_tensor(onehot[:, S], steps[:, 0:E].unsqueeze(1).unsqueeze(1).to_broadcast([P, 4, 2, E]),
                                     top_f[:, S, :].unsqueeze(3).to_broadcast([P, 4, 2, E]), ALU.is_equal))
                dve.wait_ge(gexp_ready, s + 1)
                link(V.tensor_scalar(gsum[:, S], gexp[:, S], 1.0, None, ALU.add))
                link(V.reciprocal(grec[:, S], gsum[:, S]))
                link(V.tensor_scalar(gw[:, S, 0], grec[:, S], 2.0 / WS, None, ALU.mult))
                link(V.tensor_tensor(gw[:, S, 1], gw[:, S, 0], gexp[:, S], ALU.mult))
                link(V.tensor_tensor(onehot[:, S], onehot[:, S], gw[:, S, :].unsqueeze(3).to_broadcast([P, 4, 2, E]), ALU.mult))
                link(V.tensor_tensor(gates[:, S, :], onehot[:, S, 0, :], onehot[:, S, 1, :], ALU.add))
                for t in range(s * 4, s * 4 + 4):
                    at = (t % 2) * AW
                    ins = V.tensor_tensor(gated_h[:, t, :].rearrange("p (e r) -> p e r", e=E),
                                          ps(("aw", t // 2))[:, at:at + P].rearrange("p (e r) -> p e r", e=E),
                                          gates[:, t, :].unsqueeze(2).to_broadcast([P, E, R]), ALU.mult)
                    if t % 2 == 1:
                        ins.then_inc(free_of(("aw", t // 2)), 1)

            def gh_low(i):
                dve.wait_ge(gt_hi, i + 1)
                V.tensor_tensor(gh16[:, 1, 2 * i:2 * i + 2, :], ps(("gt", i))[:, 0:2 * P].rearrange("p (t n) -> p t n", t=2),
                                gh16[:, 0, 2 * i:2 * i + 2, :], ALU.subtract).then_inc(free_of(("gt", i)), 1)

            def x3t_low(t):
                dve.wait_ge(x3t_hi, t + 1)
                V.tensor_tensor(xt16[:, 1, :, t * P:(t + 1) * P], ps(("x3t", t))[:, :].rearrange("p (k n) -> p k n", k=KC),
                                xt16[:, 0, :, t * P:(t + 1) * P], ALU.subtract).then_inc(free_of(("x3t", t)), 1)

            def mask_conv(t, key, c0, c1):
                await_unit(dve, key)
                if t >= 2:
                    dve.wait_ge(out_ready, t - 1)
                falling = slice(T - 1 - c0, T - 1 - c1 if c1 < T else None, -1)
                V.tensor_tensor(conv_out[:, t % 2, c0:c1], ps(key)[:, falling], conv_mask[:, c0:c1],
                                ALU.mult).then_inc(free_of(key), 1)

            for i in range(1, NT + 3):
                if i in turn_step:
                    gh_low(turn_step.index(i))
                if 2 <= i < NT + 2:
                    x3t_low(i - 2)
                if 3 <= i < NT + 2:
                    mask_conv(i - 3, ("conv", i - 3), 0, T)
            t = NT - 1
            mask_conv(t, ("conv", (t, 0)), 0, T // 2)
            mask_conv(t, ("conv", (t, 1)), T // 2, T)
            await_read(dve, ("conv", (t, 1)))
            dve.wait_ge(out_put[t % 4], 16 * (t // 4))
            V.tensor_tensor(out_sb[:, t % 4, T // 2:T], conv_out[:, t % 2, T // 2:T], x_sb[:, t, T // 2:T],
                            ALU.add).then_inc(last_ready, 1)

        @block.tensor
        def _(pe):
            mm = nc.tensor.matmul

            def transposes(key, sources, width, rows=P):
                claim(pe, key)
                for i, src in enumerate(sources):
                    last = nc.tensor.transpose(ps(key)[:, i * width:(i + 1) * width], src, ident[0:rows, 0:rows])
                last.then_inc(full_of(key), 1)

            pe.wait_ge(lora_zeroed, 1)
            for _ in range(WARM):
                mm(bank[0][:, :], lora_h16[:, 0, 0, 0:P], lora_h16[:, 0, 0:2, :].rearrange("p j n -> p (j n)"),
                   start=True, stop=True)

            pe.wait_ge(eye_added1, KC)
            for k in range(KC):
                transposes(("w1t", k), [w1_nat[:, m, k:T:KC] for m in range(KC)], P)

            for g in range(NG0):
                pe.wait_ge(w0_ready, g + 1)
                pe.wait_ge(x_in[g], 16)
                claim(pe, ("l0", g))
                for k in range(KC):
                    last = mm(ps(("l0", g))[:, k * P:(k + 1) * P], x_sb[:, g, k:T:KC], w0_diag[:, g, :],
                              start=True, stop=True)
                last.then_inc(full_of(("l0", g)), 1)
                if g == NG0 - 3:
                    pe.wait_ge(z_ready, 4)
                    pe.wait_ge(b1_in, 16)
                    claim(pe, ("z", 0))
                    nc.tensor.transpose(ps(("z", 0))[:, 2 * NH:2 * NH + KC], b1_nat, ident[0:KC, 0:KC])
                    transposes(("z", 0), [zcat[:, i].rearrange("h c n -> h (c n)") for i in range(2)], NH, NH)
            def product(dst, pairs, first=True, final=True):
                n = len(pairs) * len(PARTS_USED)
                i = 0
                for lhs, rhs in pairs:
                    for a, b in PARTS_USED:
                        last = mm(dst, lhs(a), rhs(b), start=first and i == 0, stop=final and i == n - 1)
                        i += 1
                return last

            def l1_main(m, n):
                key = ("l1", (m, n))
                claim(pe, key)
                M = slice(m * P, (m + 1) * P)
                for k in range(KC):
                    if (m, n) == (0, 0):
                        await_read(pe, ("w1t", k))
                    product(ps(key)[:, :], [(lambda a: w1t[:, a, k, M], lambda b: xt16[:, b, k, n * HALF:(n + 1) * HALF])],
                            first=(k == 0), final=False)

            def l1_lora(m, n):
                key = ("l1", (m, n))
                M = slice(m * P, (m + 1) * P)
                per = HALF // TA
                for j in range(n * per, (n + 1) * per):
                    pe.wait_ge(lb_ready, j + 1)
                    pe.wait_ge(lh_ready, j // 2 + 1)
                    c = (j - n * per) * TA
                    pairs = [(lambda a: lb16[:, a, j, M], lambda b: lora_h16[:, b, j, :])]
                    last = product(ps(key)[:, c:c + TA], pairs, first=False, final=(j == (n + 1) * per - 1))
                last.then_inc(full_of(key), 1)

            for g in range(NG0 // 2):
                await_read(pe, ("l0", g))
            for m in range(KC):
                l1_main(m, 0)
            for g in range(NG0 // 2, NG0):
                await_read(pe, ("l0", g))
            l1_main(0, 1)
            for j in range(NGA):
                key = ("la", j // 2)
                pe.wait_ge(la_ready, j + 1)
                if j % 2 == 0:
                    claim(pe, key)
                c = (j % 2) * P
                for k in range(KC):
                    for n, (a, b) in enumerate(PARTS_USED):
                        for q in range(2):
                            b0 = j * GA + q * G0
                            last = mm(ps(key)[q * N:(q + 1) * N, c:c + P],
                                      la16[:, a, k, b0:b0 + G0, :].rearrange("p b r -> p (b r)"),
                                      xt16[:, b, k, b0 * NH:b0 * NH + P], start=(k == 0 and n == 0),
                                      stop=(k == KC - 1 and n == 2))
                if j % 2 == 1:
                    last.then_inc(full_of(key), 1)
            l1_main(1, 1)
            for m in range(KC):
                l1_lora(m, 0)
            l1_lora(0, 1)
            l1_lora(1, 1)
            pe.wait_ge(eye_added2, KC)
            for k in range(2):
                transposes(("w2t", k), [w2_nat[:, m, k * P:(k + 1) * P] for m in range(KC)], P)
            l1_main(2, 1)
            l1_lora(2, 1)
            pe.wait_ge(z_ready, 5)
            transposes(("z", 1), [zcat[:, i].rearrange("h c n -> h (c n)") for i in range(2, 4)], NH, NH)
            pe.wait_ge(a2_in, 32)
            transposes(("a2t", 0), [a2_nat[:, k * P:(k + 1) * P] for k in range(KC)], P)
            transposes(("wrt", 0), [wr_nat[:, k * P:(k + 1) * P] for k in range(KC)], E, E)
            l1_main(3, 1)
            l1_lora(3, 1)
            for k in range(2, KC):
                transposes(("w2t", k), [w2_nat[:, m, k * P:(k + 1) * P] for m in range(KC)], P)
            pe.wait_ge(b2_in, 16 * KC)
            transposes(("b2t", 0), [b2_nat[:, k].rearrange("p e r -> p (e r)") for k in range(KC)], P)
            pe.wait_ge(pq_ready, 2)
            for s in range(2):
                claim(pe, ("k", s))
                for h in range(NH // 2):
                    hh = s * (NH // 2) + h
                    last = mm(ps(("k", s))[0:LA, h * LB:(h + 1) * LB], cos_a[:, hh, :], trig_b[:, hh, :],
                              start=True, stop=True)
                last.then_inc(full_of(("k", s)), 1)

            def x2_part(a, k, t):
                return x2t16[:, a, k, t * HT:(t + 1) * HT, :].rearrange("p h b -> p (h b)")

            def down(t):
                key = ("aw", t // 2)
                if t % 2 == 0:
                    claim(pe, key)
                at = (t % 2) * AW
                for k in range(KC):
                    if t == 0 and k < KC - 1:
                        pe.wait_ge(x2_ready, KC + k + 1)
                    elif t == 0:
                        pe.wait_ge(x2_last, 1)
                    last = product(ps(key)[:, at:at + AW],
                                   [(lambda a: x2_part(a, k, t), lambda b: awt[:, b, k, :])],
                                   first=(k == 0), final=(k == KC - 1))
                if t % 2 == 1:
                    last.then_inc(full_of(key), 1)

            def main2(t):
                key = ("l2", t)
                claim(pe, key)
                product(ps(key)[:, :], [(lambda a, k=k: x2_part(a, k, t), lambda b, k=k: w2t[:, b, k, :])
                                        for k in range(KC)], final=False)

            def turn_gated(i):
                claim(pe, ("gt", i))
                await_read(pe, ("aw", i))
                transposes(("gt", i), [gated_h[:, 2 * i + n, :] for n in range(2)], P)

            def up(t):
                await_read(pe, ("gt", t // 2))
                product(ps(("l2", t))[:, :], [(lambda a: gh16[:, a, t, :], lambda b: b2t[:, b, :])],
                        first=False).then_inc(full_of(("l2", t)), 1)

            def turn3(t):
                await_read(pe, ("l2", t))
                transposes(("x3t", t), [x_sb[:, t, k * P:(k + 1) * P] for k in range(KC)], P)

            def conv(t, key, c0, c1):
                claim(pe, key)
                await_read(pe, ("x3t", t))
                pe.wait_ge(toep_in[t], 16)
                chunks = [k for k in range(KC) if c0 < T - k * P]
                for k in chunks:
                    end = min(c1, T - k * P)
                    for n, (a, b) in enumerate(PARTS_USED):
                        for h in range(HT):
                            rows = slice(h * NB, (h + 1) * NB)
                            last = mm(ps(key)[rows, c0:end], xt16[:, a, k, t * P + h * NB:t * P + (h + 1) * NB],
                                      toep[:, t * HT + h, b, k * P + c0:k * P + end], start=(k == 0 and n == 0),
                                      stop=(k == chunks[-1] and n == 2))
                last.then_inc(full_of(key), 1)

            for key in [("a2t", 0), ("wrt", 0)]:
                await_read(pe, key)
            for t in range(NT // 2):
                down(t)
            for key in [("w2t", k) for k in range(KC)] + [("b2t", 0)]:
                await_read(pe, key)
            main2(0)
            for t in range(NT // 2, NT):
                down(t)
            main2(1)
            for i in range(1, NT + 3):
                if i in turn_step:
                    turn_gated(turn_step.index(i))
                if i + 1 < NT:
                    main2(i + 1)
                if i <= NT:
                    up(i - 1)
                if 2 <= i <= NT + 1:
                    turn3(i - 2)
                if 3 <= i < NT + 2:
                    conv(i - 3, ("conv", i - 3), 0, T)
            conv(NT - 1, ("conv", (NT - 1, 0)), T // 2, T)
            conv(NT - 1, ("conv", (NT - 1, 1)), 0, T // 2)


_INS = ['x', 'itok_B_0_15', 'itok_B_0_23', 'itok_B_0_7', 'itok_B_8_3872', 'L0_cond_weights', 'L1_cond_W', 'L1_cond_b',
        'L1_cond_lora_As', 'L1_cond_lora_Bs', 'L2_cond_W', 'L2_cond_Wr', 'L2_cond_A', 'L2_cond_B', 'L3_cond_log_dt',
        'L3_cond_C', 'L3_cond_log_A_real', 'L3_cond_A_imag', 'L3_cond_D']


def kernel(**inputs):
    import numpy as _np
    import concourse.bacc as _bacc
    from concourse import mybir as _mybir
    from concourse.bass_utils import run_bass_kernel_spmd as _run

    nc = _bacc.Bacc("TRN2", target_bir_lowering=False, num_devices=1)
    arrays, args = {}, []
    for name in _INS:
        a = _np.ascontiguousarray(inputs[name])
        arrays[f"in_{name}_dram"] = a
        args.append(nc.dram_tensor(f"in_{name}_dram", a.shape, _mybir.dt.from_np(a.dtype), kind="ExternalInput").ap())
    shape = arrays["in_x_dram"].shape
    args.append(nc.dram_tensor("out_0_dram", shape, _mybir.dt.float32, kind="ExternalOutput").ap())
    cond_resid_kernel(nc, *args)
    r = _run(nc, [arrays], core_ids=[0])
    return r.results[0]["out_0_dram"]
```
